# Optimizing a Trainium2 kernel written in Bass

```python
import numpy as np
import jax
import jax.numpy as jnp

def _softmax(x, axis=-1):
    return jax.nn.softmax(x, axis=axis)

def _gelu(x):
    return jax.nn.gelu(x, approximate=True)

def _silu(x):
    return jax.nn.silu(x)

def _sigmoid(x):
    return jax.nn.sigmoid(x)

def _layernorm(x, axis=-1, eps=1e-05):
    m = jnp.mean(x, axis=axis, keepdims=True)
    v = jnp.var(x, axis=axis, keepdims=True)
    return (x - m) / jnp.sqrt(v + eps)

def _scatter_add(tgt, idx, src, axis=0):
    return tgt.at[idx].add(src)

def _segment_sum(src, seg, n):
    return jax.ops.segment_sum(src, seg, n)
kernel_name = 'mk_rec_standalone_d1_rec_r8_69d5db'

def setup_inputs(seed: int=0):
    np.random.seed(seed)
    _w = jnp.asarray

    def _rec_inputs():
        import jax
        import jax.numpy as jnp
        _rk = jax.random.key(seed)
        r_target_item = -9.80646e-05 + 1.00041 * jax.random.normal(jax.random.fold_in(_rk, 1), (2048, 64), jnp.float32)
        r_history_sequence = -9.97791e-05 + 0.999858 * jax.random.normal(jax.random.fold_in(_rk, 2), (2048, 200, 64), jnp.float32)
        r_mask = jax.random.randint(jax.random.fold_in(_rk, 3), (2048, 1, 200), 0, 2, jnp.int32)
        return (r_target_item, r_history_sequence, r_mask)
    r_target_item, r_history_sequence, r_mask = _rec_inputs()

    def _L0_rec_setup():
        import jax, jax.numpy as jnp
        import numpy as np
        INPUT_DIM = 64
        ATTN_DIM = 128
        SCALE = ATTN_DIM ** 0.5
        key = jax.random.key(seed)
        k1, k2, k3, k4, k5, k6, k7 = jax.random.split(key, 7)
        B, L = (1024, 200)
        target_item = jax.random.normal(k1, (B, INPUT_DIM), dtype=jnp.float32)
        history_sequence = jax.random.normal(k2, (B, L, INPUT_DIM), dtype=jnp.float32)
        mask = jax.random.randint(k3, (B, 1, L), 0, 2, dtype=jnp.int32)
        s = 1.0 / np.sqrt(INPUT_DIM)
        W_q = jax.random.normal(k4, (INPUT_DIM, ATTN_DIM), dtype=jnp.float32) * s
        W_k = jax.random.normal(k5, (INPUT_DIM, ATTN_DIM), dtype=jnp.float32) * s
        W_v = jax.random.normal(k6, (INPUT_DIM, ATTN_DIM), dtype=jnp.float32) * s
        W_o = jax.random.normal(k7, (ATTN_DIM, INPUT_DIM), dtype=jnp.float32) * (1.0 / np.sqrt(ATTN_DIM))
        return {'target_item': target_item, 'history_sequence': history_sequence, 'mask': mask, 'W_q': W_q, 'W_k': W_k, 'W_v': W_v, 'W_o': W_o}
    _L0_rec_all = _L0_rec_setup()
    _L0_rec_in = {k: v for k, v in _L0_rec_all.items() if k in ('W_q', 'W_k', 'W_v', 'W_o')}
    del _L0_rec_all
    return {'r_target_item': r_target_item, 'r_history_sequence': r_history_sequence, 'r_mask': r_mask, 'L0_rec_W_q': _L0_rec_in['W_q'], 'L0_rec_W_k': _L0_rec_in['W_k'], 'L0_rec_W_v': _L0_rec_in['W_v'], 'L0_rec_W_o': _L0_rec_in['W_o']}

def reference(r_target_item, r_history_sequence, r_mask, L0_rec_W_q, L0_rec_W_k, L0_rec_W_v, L0_rec_W_o):
    import jax
    import jax.numpy as jnp

    def _L0_rec_ref(target_item, history_sequence, mask, W_q, W_k, W_v, W_o):
        import jax, jax.numpy as jnp
        import numpy as np
        INPUT_DIM = 64
        ATTN_DIM = 128
        SCALE = ATTN_DIM ** 0.5
        Q = target_item @ W_q
        K = jnp.einsum('bld,da->bla', history_sequence, W_k)
        V = jnp.einsum('bld,da->bla', history_sequence, W_v)
        scores = jnp.einsum('ba,bla->bl', Q, K) / SCALE
        scores = scores * mask[:, 0, :].astype(scores.dtype)
        attention = jax.nn.relu(scores)
        out = jnp.einsum('bl,bla->ba', attention, V)
        out = out @ W_o + target_item
        return out
    y = _L0_rec_ref(r_target_item, r_history_sequence, r_mask, L0_rec_W_q, L0_rec_W_k, L0_rec_W_v, L0_rec_W_o)
    return y

_drawn_inputs = setup_inputs


def setup_inputs(seed=0):
    import zlib

    import numpy as np

    out = dict(_drawn_inputs(seed))
    spreads = {}
    factors = {}
    for name, (base, spread) in spreads.items():
        noise = np.random.default_rng([zlib.crc32(name.encode()), seed]).standard_normal(out[name].shape)
        drawn = base * np.exp(spread * noise) if base else spread * noise
        out[name] = jnp.asarray(drawn.astype(out[name].dtype))
    for name, factor in factors.items():
        out[name] = (out[name] * factor).astype(out[name].dtype)
    return out
```

```python
from contextlib import ExitStack

import concourse.bass as bass
from concourse import mybir

F32 = mybir.dt.float32
I32 = mybir.dt.int32
ALU = mybir.AluOpType
ACT = mybir.ActivationFunctionType
AX_X = mybir.AxisListType.X

P = 128
B, L, D, A = 2048, 200, 64, 128
SCALE = float(A) ** 0.5
WINDOWS = B // P
TILES, STEPS, PAIRS, PAR = 4, 4, 4, 2
TP = STEPS * PAIRS
L0, L1, LR = 128, 64, 8
COLS = P // TILES
CUTS = ((0, L0), (2 * L0, L1), (2 * (L0 + L1), LR))

C_ID, C_SELS, C_SELC, C_SELD, C_SELE, C_SEL1, C_SELR, C_END = 0, 128, 130, 138, 146, 148, 212, 244

ACT_FILLS = [(f"F{f}", s, bank) for s in range(STEPS) for f, bank in ((0, 0), (1, 1), (3, 0), (4, 1))]
ACT_N = len(ACT_FILLS)
DVE_FILLS = [("F2", 0, 0), ("F5", 0, 1), ("F2", 1, 0), ("F5", 1, 1), ("F2", 2, 0), ("F5", 2, 1),
             ("F2", 3, 0), ("CT", 3, 1), ("F5", 3, 0), ("OUT", 3, 1), ("FR", 3, 0)]
DVE_N = len(DVE_FILLS)


def attention_kernel(nc, target, history, mask, wq, wk, wv, wo, consts, out):
    with ExitStack() as ctx:
        def sb(name, shape, dt=F32):
            return ctx.enter_context(nc.sbuf_tensor(name, shape, dt))

        def bank(name):
            return ctx.enter_context(nc.psum_tensor(name, [P, 512], F32))

        def sem(name):
            return ctx.enter_context(nc.semaphore(name))

        hist = sb("hist", [P, STEPS, TILES, 2, 2 * L])
        h0 = sb("h0", [P, STEPS, TILES, PAIRS * P])
        h1 = sb("h1", [P, TILES, STEPS, 2 * P])
        hr = sb("hr", [P, TILES, P])
        rest = sb("rest", [P, TILES, TP, LR])
        g_all = sb("g_all", [P, B])
        g_cols = sb("g_cols", [P, TILES, STEPS, 2, COLS])
        tgt = sb("tgt", [P, WINDOWS, D])
        tgt_t = sb("tgt_t", [D, B])
        msk = sb("msk", [P, L], I32)
        const = sb("const", [P, C_END])
        w0 = sb("w0", [P, TILES, STEPS, COLS])
        w1 = sb("w1", [P, 2, TILES, COLS])
        wr = sb("wr", [P, TILES, COLS])
        msk_own = sb("msk_own", [P, 2 * L])
        masked = sb("masked", [P, 2 * L])
        att = sb("att", [P, 3 * P])
        picked = sb("picked", [P, 18, D])
        csum = sb("csum", [P, P])
        csum_t = sb("csum_t", [D, P])
        wq_s, wk_s, wv_s = sb("wq_s", [D, A]), sb("wk_s", [D, A]), sb("wv_s", [D, A])
        wo_s = sb("wo_s", [A, D])
        w_t = sb("w_t", [A, 3, D])
        m_score = sb("m_score", [D, 2, D])
        m_out = sb("m_out", [D, D])

        ps_score, ps_c0, ps_c1, ps_misc = bank("ps_score"), bank("ps_c0"), bank("ps_c1"), bank("ps_misc")
        ba = [bank("ba0"), bank("ba1")]
        bd = [bank("bd0"), bank("bd1")]
        ps_at = ps_misc[:, 0:3 * P]
        ps_cr = ps_misc[:, 3 * P:4 * P]

        ident = const[:, C_ID:C_ID + P]

        loaded = [sem(f"hist_loaded{s}") for s in range(STEPS)]
        small_loaded, tgt_loaded, msk_loaded = sem("small_loaded"), sem("tgt_loaded"), sem("msk_loaded")
        out_stored = sem("out_stored")
        zeroed = sem("zeroed")
        prep_pe, prep_done = sem("prep_pe"), sem("prep_done")
        g_placed = sem("g_placed")
        rest_copied = sem("rest_copied")
        scored = sem("scored")
        msk_placed, masked_done, att_ready = sem("msk_placed"), sem("masked_done"), sem("att_ready")
        at_done = sem("at_done")
        weights_placed = sem("weights_placed")
        ctx_done, ctx_read = sem("ctx_done"), sem("ctx_read")
        csum_ready = sem("csum_ready")
        act_filled, act_emptied = sem("act_filled"), sem("act_emptied")
        dve_filled, dve_emptied = sem("dve_filled"), sem("dve_emptied")

        def index(fills, name, s):
            return next(i for i, x in enumerate(fills) if x[0] == name and x[1] == s)

        def ge(eng, s, value):
            if not isinstance(value, int) or value > 0:
                eng.wait_ge(s, value)

        block = ctx.enter_context(nc.Block())

        @block.sync
        def _(sp):
            def value(x):
                return x if isinstance(x, int) else sp.snap(x)

            def load(block, s):
                sp.dma_start(hist[:, s].rearrange("p t q l -> p (t q l)"),
                             history[bass.ds(block, 1)].rearrange("o p n -> (o p) n")).then_inc(loaded[s], 16)

            def load_mask(row):
                sp.dma_start(msk[:], mask[bass.ds(row, P), :]).then_inc(msk_loaded, 16)

            def store(w, row):
                sp.dma_start(out[bass.ds(row, P), :], tgt[:, bass.ds(w, 1), :].rearrange("p o d -> p (o d)")).then_inc(out_stored, 16)

            def window(w):
                last = w - 1
                for s in range(STEPS):
                    if s == STEPS - 1:
                        row, placed = value(w * P), value(w)
                        sp.wait_ge(msk_placed, placed)
                        load_mask(row)
                    block = value(w * STEPS + s)
                    filled = value(last * DVE_N + index(DVE_FILLS, "F5", s) + 1)
                    sp.wait_ge(dve_filled, filled)
                    load(block, s)

            for dst, src in ((wq_s, wq), (wk_s, wk), (wv_s, wv), (wo_s, wo), (const, consts)):
                sp.dma_start(dst[:], src).then_inc(small_loaded, 16)
            sp.dma_start(tgt[:], target.rearrange("(w p) d -> p w d", p=P)).then_inc(tgt_loaded, 16)
            for s in range(STEPS):
                load(s, s)
            load_mask(0)
            window(1)
            with sp.Fori(2, WINDOWS) as w:
                window(w)
                w2, row = value(w - 2), value((w - 2) * P)
                complete = value((w - 1) * DVE_N + index(DVE_FILLS, "OUT", STEPS - 1) + 1)
                sp.wait_ge(dve_emptied, complete)
                store(w2, row)
            sp.wait_ge(dve_emptied, (WINDOWS - 1) * DVE_N + index(DVE_FILLS, "OUT", STEPS - 1) + 1)
            store(WINDOWS - 2, (WINDOWS - 2) * P)
            sp.wait_ge(dve_emptied, WINDOWS * DVE_N + 2)
            store(WINDOWS - 1, (WINDOWS - 1) * P)
            sp.wait_ge(out_stored, 16 * WINDOWS)

        @block.gpsimd
        def _(pool):
            nc.gpsimd.memset(g_cols[:], 0.0).then_inc(zeroed, 1)
            nc.gpsimd.memset(w0[:], 0.0).then_inc(zeroed, 1)

        @block.scalar
        def _(act):
            def place_g(w):
                for par in range(PAR):
                    rows = slice(par * D, (par + 1) * D)
                    if isinstance(w, int):
                        src = g_all[rows, w * P:(w + 1) * P]
                    else:
                        src = g_all[rows, bass.ds(w * P, P)]
                    src = src.rearrange("p (t u i r) -> p t u i r", t=TILES, u=STEPS * 2, i=2)[:, :, :, :, par]
                    flat = g_cols[rows].rearrange("p t s q c -> p t (s q c)")
                    dst = bass.AP(flat.tensor, flat.offset + par,
                                  [flat.ap[0], [STEPS * 2 * COLS, TILES], [COLS + 4, STEPS * 2], [2, 2]])
                    last = nc.scalar.copy(dst, src)
                last.then_inc(g_placed, 1)

            def place_mask(w):
                act.wait_ge(msk_loaded, (w + 1) * 16)
                ge(act, masked_done, w)
                at = 0
                for cut, n in CUTS:
                    for i in range(2):
                        last = nc.scalar.activation(msk_own[:, cut + i * n:cut + (i + 1) * n], msk[:, at:at + n], ACT.Copy,
                                                    scale=const[:, C_SELS + i:C_SELS + i + 1])
                    at += n
                last.then_inc(msk_placed, 1)

            def copy_rest(w, s):
                act.wait_ge(loaded[s], (w + 1) * 16)
                if s == 0:
                    ge(act, dve_filled, w * DVE_N)
                nc.scalar.copy(rest[:, :, s * PAIRS:(s + 1) * PAIRS, :].rearrange("p t (q i) l -> p t q (i l)", i=2),
                               hist[:, s, :, :, 2 * (L0 + L1):2 * L]).then_inc(rest_copied, 1)

            def window(w, more):
                k = 0
                for name, s, b in ACT_FILLS:
                    if name == "F0" and s == STEPS - 1 and more:
                        act.wait_ge(scored, w + 1)
                        place_g(w + 1)
                    if name == "F3":
                        copy_rest(w, s)
                        if s == 0:
                            place_mask(w)
                    k += 1
                    act.wait_ge(act_filled, w * ACT_N + k)
                    if name == "F4":
                        dst = h1[:, 0:2, s, :]
                        src = ba[b][:].rearrange("p (t n) -> p t n", t=2)
                    else:
                        dst = h0[:, s, int(name[1]), :]
                        src = ba[b][:]
                    nc.scalar.copy(dst, src).then_inc(act_emptied, 1)

            act.wait_ge(zeroed, 2)
            act.wait_ge(small_loaded, 16 * 5)
            act.wait_ge(prep_done, 4)
            place_g(0)
            window(0, True)
            with act.Fori(1, WINDOWS - 1) as w:
                window(w, True)
            window(WINDOWS - 1, False)

        @block.vector
        def _(dve):
            dve.wait_ge(zeroed, 2)
            dve.wait_ge(prep_pe, 1)
            nc.vector.tensor_copy(w_t[:].rearrange("a k d -> a (k d)"), ba[0][:, 0:3 * D]).then_inc(prep_done, 1)
            dve.wait_ge(prep_pe, 2)
            nc.vector.tensor_scalar(m_score[:], ba[1][0:D, 0:D].rearrange("p (o d) -> p o d", o=1).broadcast_to([D, 2, D]),
                                    1.0 / SCALE, None, ALU.mult)
            nc.vector.tensor_copy(m_out[:], ba[1][0:D, D:2 * D]).then_inc(prep_done, 1)
            for q in range(4):
                dve.wait_ge(prep_pe, 3 + q)
                r = nc.vector.tensor_copy(tgt_t[:, q * 512:(q + 1) * 512], (ba + bd)[q][0:D, :])
            r.then_inc(prep_done, 1)
            for q in range(4):
                dve.wait_ge(prep_pe, 7 + q)
                r = nc.vector.tensor_copy(g_all[:, q * 512:(q + 1) * 512], (ba + bd)[q][:])
            r.then_inc(prep_done, 1)

            def window(w, sums):
                base, fills = w * DVE_N, DVE_FILLS

                def empty(name, s):
                    i = index(fills, name, s)
                    b = fills[i][2]
                    dve.wait_ge(dve_filled, base + i + 1)
                    if name == "F2":
                        op = nc.vector.tensor_copy(h0[:, s, 2, :], bd[b][:])
                    elif name == "F5":
                        op = nc.vector.tensor_copy(h1[:, 2:4, s, :], bd[b][:].rearrange("p (t n) -> p t n", t=2))
                    elif name == "FR":
                        op = nc.vector.tensor_copy(hr[:].rearrange("p t n -> p (t n)"), bd[b][:])
                    elif name == "CT":
                        op = nc.vector.tensor_copy(csum_t[:], bd[b][0:D, 0:P])
                    op.then_inc(dve_emptied, 1)

                for s in range(STEPS - 1):
                    empty("F2", s)
                    if s == STEPS - 2 and sums:
                        pick(w)
                    empty("F5", s)
                s = STEPS - 1
                dve.wait_ge(scored, w + 1)
                dve.wait_ge(msk_placed, w + 1)
                nc.vector.tensor_tensor(masked[:], ps_score[:, 0:2 * L], msk_own[:], ALU.mult).then_inc(masked_done, 1)
                dve.wait_ge(masked_done, w + 1)
                for k, (cut, n) in enumerate(CUTS):
                    a, b = (masked[:, cut + i * n:cut + (i + 1) * n].rearrange("p (o l) -> p o l", o=1).broadcast_to([P, P // n, n])
                            for i in range(2))
                    op = nc.vector.tensor_tensor(att[:, k * P:(k + 1) * P].rearrange("p (o l) -> p o l", l=n), a, b, ALU.add)
                op.then_inc(att_ready, 1)
                empty("F2", s)
                empty("CT", s)
                dve.wait_ge(at_done, w + 1)
                flat = w0[:].rearrange("p t s c -> p t (s c)")
                dst = bass.AP(flat.tensor, flat.offset, [flat.ap[0], [STEPS * COLS, TILES], [COLS + 8, STEPS], [1, 8]])
                nc.vector.tensor_scalar(dst, ps_at[:, 0:P].rearrange("p (t s k) -> p t s k", t=TILES, s=STEPS),
                                        0.0, None, ALU.max)
                for sp_ in range(2):
                    nc.vector.scalar_tensor_tensor(
                        out=w1[:, sp_], in0=ps_at[:, P:2 * P].rearrange("p (t c) -> p t c", t=TILES), scalar=0.0,
                        in1=const[:, C_SEL1 + sp_ * COLS:C_SEL1 + (sp_ + 1) * COLS].rearrange("p (o c) -> p o c", o=1).broadcast_to([P, TILES, COLS]),
                        op0=ALU.max, op1=ALU.mult)
                nc.vector.scalar_tensor_tensor(
                    out=wr[:], in0=ps_at[:, 2 * P:3 * P].rearrange("p (t c) -> p t c", t=TILES), scalar=0.0,
                    in1=const[:, C_SELR:C_SELR + COLS].rearrange("p (o c) -> p o c", o=1).broadcast_to([P, TILES, COLS]),
                    op0=ALU.max, op1=ALU.mult).then_inc(weights_placed, 1)
                empty("F5", s)
                finish(w, base + index(fills, "OUT", s) + 1)
                empty("FR", s)

            def pick(w):
                dve.wait_ge(ctx_done, w)
                for at, n, ps, c in ((0, 8, ps_c0[:], C_SELC), (8, 8, ps_c1[:], C_SELD), (16, 2, ps_cr, C_SELE)):
                    r = nc.vector.tensor_tensor(picked[:, at:at + n, :], ps.rearrange("p (k d) -> p k d", d=D),
                                                const[:, c:c + n].rearrange("p (k o) -> p k o", o=1).broadcast_to([P, n, D]),
                                                ALU.mult)
                    r.then_inc(ctx_read, 1)
                dve.wait_ge(ctx_read, w * 3)
                nc.vector.tensor_reduce(csum[:, 0:D], picked[:].rearrange("p k d -> p d k"), AX_X, ALU.add).then_inc(csum_ready, 1)

            def finish(w, filled):
                dve.wait_ge(dve_filled, filled)
                if isinstance(w, int) and w == 0:
                    nc.vector.tensor_copy(picked[:, 0, :], bd[1][:, 0:D]).then_inc(dve_emptied, 1)
                    return
                last = w - 1
                t = tgt[:, last, :] if isinstance(last, int) else tgt[:, bass.ds(last, 1), :].rearrange("p o d -> p (o d)")
                op = nc.vector.tensor_tensor(t, bd[1][:, 0:D], t, ALU.add)
                op.then_inc(dve_emptied, 1)

            nc.vector.memset(csum[:], 0.0).then_inc(csum_ready, 1)
            window(0, False)
            with dve.Fori(1, WINDOWS) as w:
                window(w, True)
            pick(WINDOWS)
            n = WINDOWS * DVE_N
            dve.wait_ge(dve_filled, n + 1)
            nc.vector.tensor_copy(csum_t[:], bd[1][0:D, 0:P]).then_inc(dve_emptied, 1)
            finish(WINDOWS, n + 2)

        @block.tensor
        def _(pe):
            pe.wait_ge(small_loaded, 16 * 5)
            for k, m in enumerate((wq_s, wk_s, wv_s)):
                r = nc.tensor.transpose(ba[0][:, k * D:(k + 1) * D], m[:], ident[0:D, 0:D])
            r.then_inc(prep_pe, 1)
            pe.wait_ge(prep_done, 1)
            nc.tensor.matmul(ba[1][0:D, 0:D], w_t[:, 0, :], w_t[:, 1, :], start=True, stop=True)
            nc.tensor.matmul(ba[1][0:D, D:2 * D], w_t[:, 2, :], wo_s[:], start=True, stop=True).then_inc(prep_pe, 1)
            pe.wait_ge(prep_done, 2)
            pe.wait_ge(tgt_loaded, 16)
            for q in range(4):
                for j in range(4):
                    r = nc.tensor.transpose((ba + bd)[q][0:D, j * P:(j + 1) * P], tgt[:, q * 4 + j, :], ident)
                r.then_inc(prep_pe, 1)
            pe.wait_ge(prep_done, 3)
            for q in range(4):
                nc.tensor.matmul((ba + bd)[q][:], m_score[:].rearrange("p o d -> p (o d)"),
                                 tgt_t[:, q * 512:(q + 1) * 512], start=True, stop=True).then_inc(prep_pe, 1)

            def score(w, s, q):
                if q == 0:
                    pe.wait_ge(loaded[s], (w + 1) * 16)
                if s == 0 and q == 0:
                    pe.wait_ge(g_placed, w + 1)
                    ge(pe, masked_done, w)
                for t in range(TILES):
                    r = nc.tensor.matmul(ps_score[t * COLS:(t + 1) * COLS, 0:2 * L], g_cols[:, t, s, q, :],
                                         hist[:, s, t, q, :],
                                         start=(s == 0 and q == 0), stop=(s == STEPS - 1 and q == 1),
                                         tile_position=(0, t * COLS))
                if s == STEPS - 1 and q == 1:
                    r.then_inc(scored, 1)

            def sum0(w, s):
                pe.wait_ge(act_emptied, (w - 1) * ACT_N + 4 * s + 3)
                pe.wait_ge(dve_emptied, dve_prev(w, "F2", s))
                for t in range(TILES):
                    nc.tensor.matmul(ps_c0[t * COLS:(t + 1) * COLS, :], w0[:, t, s, :], h0[:, s, t, :],
                                     start=(s == 0), stop=(s == STEPS - 1), tile_position=(0, t * COLS))

            def sum1(w, j):
                pe.wait_ge(act_emptied, (w - 1) * ACT_N + 4 * (2 * j + 2))
                pe.wait_ge(dve_emptied, dve_prev(w, "F5", 2 * j + 1))
                for t in range(TILES):
                    nc.tensor.matmul(ps_c1[t * COLS:(t + 1) * COLS, :], w1[:, j, t, :],
                                     h1[:, t, 2 * j:2 * j + 2, :].rearrange("p s n -> p (s n)"),
                                     start=(j == 0), stop=(j == 1), tile_position=(0, t * COLS))

            def sum_rest(w):
                pe.wait_ge(dve_emptied, w * DVE_N)
                for t in range(TILES):
                    r = nc.tensor.matmul(ps_cr[t * COLS:(t + 1) * COLS, :], wr[:, t, :], hr[:, t, :],
                                         start=True, stop=True, tile_position=(0, t * COLS))
                r.then_inc(ctx_done, 1)

            def dve_prev(w, name, s):
                return (w - 1) * DVE_N + index(DVE_FILLS, name, s) + 1

            def before_sums(w):
                pe.wait_ge(weights_placed, w)
                ge(pe, ctx_read, (w - 1) * 3)

            def act_bank(w, name, s):
                i = index(ACT_FILLS, name, s)
                ge(pe, act_emptied, w * ACT_N + i - 1)
                return ba[ACT_FILLS[i][2]]

            def dve_bank(w, name, s):
                fills = DVE_FILLS
                i = index(fills, name, s)
                b = fills[i][2]
                before = [k for k in range(i) if fills[k][2] == b]
                if before:
                    value = w * DVE_N + before[-1] + 1
                else:
                    value = w * DVE_N - b
                ge(pe, dve_emptied, value)
                return bd[b]

            def turn0(w, s, t):
                ps = dve_bank(w, "F2", s) if t == 2 else act_bank(w, f"F{t}", s)
                for r in range(PAIRS):
                    op = nc.tensor.transpose(ps[:, r * P:(r + 1) * P], hist[:, s, t, r // 2, r % 2 * L0:(r % 2 + 1) * L0], ident)
                op.then_inc(dve_filled if t == 2 else act_filled, 1)

            def turn1(w, s, half):
                if half:
                    pe.wait_ge(rest_copied, w * STEPS + s + 1)
                ps = dve_bank(w, "F5", s) if half else act_bank(w, "F4", s)
                for k in range(4):
                    t, c = 2 * half + k // 2, k % 2
                    op = nc.tensor.transpose(ps[:, k * P:(k + 1) * P], hist[:, s, t, c, 2 * L0:2 * (L0 + L1)], ident)
                op.then_inc(dve_filled if half else act_filled, 1)

            def turn_rest(w):
                pe.wait_ge(rest_copied, (w + 1) * STEPS)
                ps = dve_bank(w, "FR", STEPS - 1)
                for t in range(TILES):
                    op = nc.tensor.transpose(ps[:, t * P:(t + 1) * P], rest[:, t, :, :].rearrange("p r l -> p (r l)"), ident)
                op.then_inc(dve_filled, 1)

            def turn_weights(w):
                pe.wait_ge(att_ready, w + 1)
                ge(pe, ctx_read, w * 3)
                for k in range(len(CUTS)):
                    op = nc.tensor.transpose(ps_at[:, k * P:(k + 1) * P], att[:, k * P:(k + 1) * P], ident)
                op.then_inc(at_done, 1)

            def csum_turn(w, b):
                pe.wait_ge(csum_ready, w + 1)
                nc.tensor.transpose(b[:, 0:P], csum[:], ident).then_inc(dve_filled, 1)

            def out_product(b, emptied):
                pe.wait_ge(dve_emptied, emptied)
                nc.tensor.matmul(b[:, 0:D], csum_t[:], m_out[:], start=True, stop=True).then_inc(dve_filled, 1)

            def window(w, sums, more):
                for s in range(STEPS):
                    last = s == STEPS - 1
                    ahead = (lambda q: score(w, s + 1, q)) if not last else (lambda q: score(w + 1, 0, q))
                    if s == 0 and sums:
                        before_sums(w)
                    if sums:
                        if s == 0:
                            sum0(w, 0)
                        elif s == 1:
                            sum0(w, 1)
                        elif s == 2:
                            sum0(w, 3)
                            sum1(w, 1)
                            sum_rest(w)
                    for t in (0, 1, 2):
                        turn0(w, s, t)
                    if sums:
                        if s == 0:
                            sum1(w, 0)
                        elif s == 1:
                            sum0(w, 2)
                    if last:
                        csum_turn(w, dve_bank(w, "CT", s))
                    if last:
                        turn_weights(w)
                    if more or not last:
                        ahead(0)
                    turn0(w, s, 3)
                    turn1(w, s, 0)
                    turn1(w, s, 1)
                    if last:
                        out_product(dve_bank(w, "OUT", s), w * DVE_N + index(DVE_FILLS, "CT", s) + 1)
                        turn_rest(w)
                    if more or not last:
                        ahead(1)

            pe.wait_ge(prep_done, 4)
            score(0, 0, 0)
            score(0, 0, 1)
            window(0, False, True)
            with pe.Fori(1, WINDOWS - 1) as w:
                window(w, True, True)
            window(WINDOWS - 1, True, False)
            w = WINDOWS
            before_sums(w)
            for s in range(STEPS):
                sum0(w, s)
            sum1(w, 0)
            sum1(w, 1)
            sum_rest(w)
            n = w * DVE_N
            csum_turn(w, bd[1])
            out_product(bd[1], n + 1)


def constants():
    import numpy as np
    c = np.zeros((P, C_END), np.float32)
    p = np.arange(P)
    c[:, C_ID:C_ID + P] = np.eye(P)
    b = p % COLS
    s, pr, par = b // 8, b // 2 % PAIRS, b % 2
    c[p, C_SELS + pr % 2] = 1
    c[p, C_SELC + pr * 2 + par] = 1
    c[p, C_SELD + (s % 2) * 4 + (pr // 2) * 2 + par] = 1
    c[p, C_SELE + par] = 1
    col = np.arange(COLS)
    for j in range(2):
        c[:, C_SEL1 + j * COLS:C_SEL1 + (j + 1) * COLS] = (col // 16 == j) & (col // 2 % 2 == (p // L1)[:, None])
    c[:, C_SELR:C_SELR + COLS] = col // 2 == (p // LR)[:, None]
    return c


def kernel(**inputs):
    import numpy as np
    import concourse.bacc as bacc
    from concourse.bass_utils import run_bass_kernel_spmd

    nc = bacc.Bacc("TRN2", target_bir_lowering=False, num_devices=1)
    hist = np.asarray(inputs["r_history_sequence"]).reshape(WINDOWS, TILES, STEPS, 2, 2, PAR, L, D)
    hist = hist.transpose(0, 2, 5, 7, 1, 3, 4, 6)
    laid, at = [], 0
    for _, n in CUTS:
        laid.append(hist[..., at:at + n].reshape(WINDOWS * STEPS, P, TILES, 2, 2 * n))
        at += n
    hist = np.concatenate(laid, axis=-1).reshape(WINDOWS * STEPS, P, TILES * 2 * 2 * L)
    arrays = {
        "target": np.ascontiguousarray(inputs["r_target_item"]),
        "history": hist,
        "mask": np.ascontiguousarray(inputs["r_mask"]).reshape(B, L),
        "wq": np.ascontiguousarray(inputs["L0_rec_W_q"]),
        "wk": np.ascontiguousarray(inputs["L0_rec_W_k"]),
        "wv": np.ascontiguousarray(inputs["L0_rec_W_v"]),
        "wo": np.ascontiguousarray(inputs["L0_rec_W_o"]),
        "consts": constants(),
    }
    args = [nc.dram_tensor(n, a.shape, mybir.dt.from_np(a.dtype), kind="ExternalInput").ap() for n, a in arrays.items()]
    out = nc.dram_tensor("out", (B, D), F32, kind="ExternalOutput").ap()
    attention_kernel(nc, *args, out)
    r = run_bass_kernel_spmd(nc, [arrays], core_ids=[0])
    return r.results[0]["out"]
```

```python
from contextlib import ExitStack

import concourse.bass as bass
from concourse import mybir

F32 = mybir.dt.float32
I32 = mybir.dt.int32
ALU = mybir.AluOpType
ACT = mybir.ActivationFunctionType
AX_X = mybir.AxisListType.X

P = 128
B, L, D, A = 2048, 200, 64, 128
SCALE = float(A) ** 0.5
BLOCKS = B // P
DIRECT = BLOCKS // 4
WINDOWS = BLOCKS - DIRECT
TILES, STEPS, PAIRS, PAR = 4, 4, 4, 2
TP = STEPS * PAIRS
L0, L1, LR = 128, 64, 8
COLS = P // TILES
CHUNKS = WINDOWS * STEPS
CHUNK = -(-L * DIRECT // CHUNKS)
BLOCK_CHUNKS = CHUNKS // DIRECT
assert CHUNK * BLOCK_CHUNKS >= L
CUTS = ((0, L0), (2 * L0, L1), (2 * (L0 + L1), LR))

C_ID, C_SELS, C_SELC, C_SELD, C_SELE, C_SEL1, C_SELR, C_END = 0, 128, 130, 138, 146, 148, 212, 244

ACT_ORDER = [(f"F{f}", s) for s in range(STEPS) for f in (0, 1, 4, 2, 3)] + [("FR", STEPS - 1)]
ACT_FILLS = [(name, s, k % 2) for k, (name, s) in enumerate(ACT_ORDER)]
DVE_FILLS = [("F5", 0, 0), ("F5", 1, 1), ("F5", 2, 0), ("CT", 3, 1), ("F5", 3, 0), ("OUT", 3, 1)]
ACT_N, DVE_N = len(ACT_FILLS), len(DVE_FILLS)


def attention_kernel(nc, target, history, direct, mask, direct_mask, wq, wk, wv, wo, consts, out):
    with ExitStack() as ctx:
        def sb(name, shape, dt=F32):
            return ctx.enter_context(nc.sbuf_tensor(name, shape, dt))

        def bank(name):
            return ctx.enter_context(nc.psum_tensor(name, [P, 512], F32))

        def sem(name):
            return ctx.enter_context(nc.semaphore(name))

        hist = sb("hist", [P, STEPS, TILES, 2, 2 * L])
        h0 = sb("h0", [P, STEPS, TILES, PAIRS * P])
        h1 = sb("h1", [P, TILES, STEPS, 2 * P])
        hr = sb("hr", [P, TILES, P])
        rest = sb("rest", [P, TILES, TP, LR])
        g_all = sb("g_all", [P, WINDOWS * P])
        g_cols = sb("g_cols", [P, TILES, STEPS, 2, COLS])
        tgt = sb("tgt", [P, BLOCKS, D])
        tgt_t = sb("tgt_t", [D, B])
        msk = sb("msk", [P, L], I32)
        const = sb("const", [P, C_END])
        w0 = sb("w0", [P, TILES, STEPS, COLS])
        w1 = sb("w1", [P, 2, TILES, COLS])
        wr = sb("wr", [P, TILES, COLS])
        msk_own = sb("msk_own", [P, 2 * L])
        masked = sb("masked", [P, 2 * L])
        att = sb("att", [P, 3 * P])
        picked = sb("picked", [P, 18, D])
        csum = sb("csum", [P, P])
        csum_t = sb("csum_t", [D, P])
        dhist = sb("dhist", [P, STEPS, CHUNK, D])
        dmask = sb("dmask", [P, WINDOWS, STEPS * CHUNK], I32)
        dg = sb("dg", [P, WINDOWS + 1, D])
        dg_now = sb("dg_now", [P, 2, D])
        by_g = sb("by_g", [P, 2, CHUNK, D])
        by_a = sb("by_a", [P, 2, CHUNK, D])
        dscore = sb("dscore", [P, CHUNK])
        dmasked = sb("dmasked", [P, CHUNK])
        datt = sb("datt", [P, 2, CHUNK])
        parts = sb("parts", [P, WINDOWS, STEPS, D])
        dsum = sb("dsum", [P, DIRECT, D])
        dsum_t = sb("dsum_t", [D, DIRECT, P])
        wq_s, wk_s, wv_s = sb("wq_s", [D, A]), sb("wk_s", [D, A]), sb("wv_s", [D, A])
        wo_s = sb("wo_s", [A, D])
        w_t = sb("w_t", [A, 3, D])
        m_score = sb("m_score", [D, 2, D])
        m_out = sb("m_out", [D, D])

        ps_score, ps_c0, ps_c1, ps_misc = bank("ps_score"), bank("ps_c0"), bank("ps_c1"), bank("ps_misc")
        ba = [bank("ba0"), bank("ba1")]
        bd = [bank("bd0"), bank("bd1")]
        ps_at = ps_misc[:, 0:3 * P]
        ps_cr = ps_misc[:, 3 * P:4 * P]

        ident = const[:, C_ID:C_ID + P]

        loaded = [[sem(f"hist_loaded{s}{half}") for half in range(2)] for s in range(STEPS)]
        small_loaded, tgt_loaded, msk_loaded = sem("small_loaded"), sem("tgt_loaded"), sem("msk_loaded")
        out_stored = sem("out_stored")
        zeroed = sem("zeroed")
        prep_pe, prep_done = sem("prep_pe"), sem("prep_done")
        g_placed = sem("g_placed")
        rest_copied = sem("rest_copied")
        scored = sem("scored")
        msk_placed, masked_done, att_ready = sem("msk_placed"), sem("masked_done"), sem("att_ready")
        at_done = sem("at_done")
        weights_placed = sem("weights_placed")
        ctx_done, ctx_read = sem("ctx_done"), sem("ctx_read")
        csum_ready = sem("csum_ready")
        dloaded = [sem(f"direct_loaded{s}") for s in range(STEPS)]
        dmask_loaded, dg_set = sem("dmask_loaded"), sem("dg_set")
        by_g_done, dscored, dmasked_done, datt_done = sem("by_g_done"), sem("dscored"), sem("dmasked_done"), sem("datt_done")
        by_a_done, part_done, dsum_done = sem("by_a_done"), sem("part_done"), sem("dsum_done")
        act_filled, act_emptied = sem("act_filled"), sem("act_emptied")
        dve_filled, dve_emptied = sem("dve_filled"), sem("dve_emptied")

        def index(fills, name, s):
            return next(i for i, x in enumerate(fills) if x[0] == name and x[1] == s)

        def ge(eng, s, value):
            if not isinstance(value, int) or value > 0:
                eng.wait_ge(s, value)

        block = ctx.enter_context(nc.Block())

        @block.sync
        def _(sp):
            def value(x):
                return x if isinstance(x, int) else sp.snap(x)

            def load(block, s, half):
                sp.dma_start(hist[:, s, 2 * half:2 * half + 2].rearrange("p t q l -> p (t q l)"),
                             history[bass.ds(block, 1), half].rearrange("o p n -> (o p) n")).then_inc(loaded[s][half], 16)

            def load_direct(block, s):
                sp.dma_start(dhist[:, s].rearrange("p l d -> p (l d)"),
                             direct[bass.ds(block, 1)].rearrange("o p n -> (o p) n")).then_inc(dloaded[s], 16)

            def load_mask(row):
                sp.dma_start(msk[:], mask[bass.ds(row, P), :]).then_inc(msk_loaded, 16)

            def store(w, row):
                sp.dma_start(out[bass.ds(row, P), :], tgt[:, bass.ds(w, 1), :].rearrange("p o d -> p (o d)")).then_inc(out_stored, 16)

            def window(w):
                last = w - 1
                for s in range(STEPS):
                    if s == STEPS - 1:
                        row, placed = value(w * P), value(w)
                        sp.wait_ge(msk_placed, placed)
                        load_mask(row)
                    block = value(w * STEPS + s)
                    filled = value(last * ACT_N + index(ACT_FILLS, "F4", s) + 1)
                    sp.wait_ge(act_filled, filled)
                    load(block, s, 0)
                    filled = value(last * DVE_N + index(DVE_FILLS, "F5", s) + 1)
                    sp.wait_ge(dve_filled, filled)
                    load(block, s, 1)
                    direct_after(last, s)

            def direct_after(w, s):
                block = value(w * STEPS + s)
                if not isinstance(w, int) or w > 0:
                    taken = value((w - 1) * STEPS + s + 1)
                    sp.wait_ge(by_a_done, taken)
                load_direct(block, s)

            for dst, src in ((wq_s, wq), (wk_s, wk), (wv_s, wv), (wo_s, wo), (const, consts)):
                sp.dma_start(dst[:], src).then_inc(small_loaded, 16)
            sp.dma_start(tgt[:], target.rearrange("(w p) d -> p w d", p=P)).then_inc(tgt_loaded, 16)
            for s in range(STEPS):
                load(s, s, 0)
                load(s, s, 1)
                if s == 0:
                    load_mask(0)
                    sp.dma_start(dmask[:], direct_mask).then_inc(dmask_loaded, 16)
            window(1)
            with sp.Fori(2, WINDOWS) as w:
                window(w)
                w2, row = value(w - 2), value((w - 2) * P)
                complete = value((w - 1) * DVE_N + index(DVE_FILLS, "OUT", STEPS - 1) + 1)
                sp.wait_ge(dve_emptied, complete)
                store(w2, row)
            for s in range(STEPS):
                direct_after(WINDOWS - 1, s)
            sp.wait_ge(dve_emptied, (WINDOWS - 1) * DVE_N + index(DVE_FILLS, "OUT", STEPS - 1) + 1)
            store(WINDOWS - 2, (WINDOWS - 2) * P)
            sp.wait_ge(dve_emptied, WINDOWS * DVE_N + 2)
            store(WINDOWS - 1, (WINDOWS - 1) * P)
            sp.wait_ge(dve_emptied, WINDOWS * DVE_N + 4)
            sp.dma_start(out[WINDOWS * P:B, :].rearrange("(w p) d -> p w d", p=P), tgt[:, WINDOWS:BLOCKS, :]).then_inc(out_stored, 16)
            sp.wait_ge(out_stored, 16 * (WINDOWS + 1))

        @block.gpsimd
        def _(pool):
            nc.gpsimd.memset(g_cols[:], 0.0).then_inc(zeroed, 1)
            nc.gpsimd.memset(w0[:], 0.0).then_inc(zeroed, 1)

            def times_g(w, s):
                n, b = w * STEPS + s, s % 2
                pool.wait_ge(dloaded[s], (w + 1) * 16)
                ge(pool, dscored, n - 1)
                pool.wait_ge(dg_set, w * 2 + b + 1)
                nc.gpsimd.tensor_tensor(by_g[:, b], dhist[:, s], dg_now[:, b].rearrange("p (o d) -> p o d", o=1).broadcast_to([P, CHUNK, D]),
                                        ALU.mult).then_inc(by_g_done, 1)

            def times_a(w, s):
                n, b = w * STEPS + s, s % 2
                pool.wait_ge(datt_done, n + 1)
                ge(pool, part_done, n - 1)
                nc.gpsimd.tensor_tensor(by_a[:, b], dhist[:, s], datt[:, b].rearrange("p (l o) -> p l o", o=1).broadcast_to([P, CHUNK, D]),
                                        ALU.mult).then_inc(by_a_done, 1)

            pool.wait_ge(prep_done, 5)
            for s in range(STEPS):
                times_g(0, s)
                if s > 0:
                    times_a(0, s - 1)
            with pool.Fori(1, WINDOWS) as w:
                for s in range(STEPS):
                    times_g(w, s)
                    if s > 0:
                        times_a(w, s - 1)
                    else:
                        times_a(w - 1, STEPS - 1)
            times_a(WINDOWS - 1, STEPS - 1)

        @block.scalar
        def _(act):
            def place_g(w):
                for par in range(PAR):
                    rows = slice(par * D, (par + 1) * D)
                    if isinstance(w, int):
                        src = g_all[rows, w * P:(w + 1) * P]
                    else:
                        src = g_all[rows, bass.ds(w * P, P)]
                    src = src.rearrange("p (t u i r) -> p t u i r", t=TILES, u=STEPS * 2, i=2)[:, :, :, :, par]
                    flat = g_cols[rows].rearrange("p t s q c -> p t (s q c)")
                    dst = bass.AP(flat.tensor, flat.offset + par,
                                  [flat.ap[0], [STEPS * 2 * COLS, TILES], [COLS + 4, STEPS * 2], [2, 2]])
                    last = nc.scalar.copy(dst, src)
                last.then_inc(g_placed, 1)

            def place_mask(w):
                act.wait_ge(msk_loaded, (w + 1) * 16)
                ge(act, masked_done, w)
                at = 0
                for cut, n in CUTS:
                    for i in range(2):
                        last = nc.scalar.activation(msk_own[:, cut + i * n:cut + (i + 1) * n], msk[:, at:at + n], ACT.Copy,
                                                    scale=const[:, C_SELS + i:C_SELS + i + 1])
                    at += n
                last.then_inc(msk_placed, 1)

            def copy_rest(w, s):
                for half in range(2):
                    act.wait_ge(loaded[s][half], (w + 1) * 16)
                if s == 0:
                    ge(act, act_filled, w * ACT_N)
                nc.scalar.copy(rest[:, :, s * PAIRS:(s + 1) * PAIRS, :].rearrange("p t (q i) l -> p t q (i l)", i=2),
                               hist[:, s, :, :, 2 * (L0 + L1):2 * L]).then_inc(rest_copied, 1)

            def window(w, more):
                k = 0
                for name, s, b in ACT_FILLS:
                    if name == "F0" and s == STEPS - 1 and more:
                        act.wait_ge(scored, w + 1)
                        place_g(w + 1)
                    if name == "F1":
                        copy_rest(w, s)
                    if name == "F3" and s == 0:
                        place_mask(w)
                    k += 1
                    act.wait_ge(act_filled, w * ACT_N + k)
                    if name == "F4":
                        dst = h1[:, 0:2, s, :]
                        src = ba[b][:].rearrange("p (t n) -> p t n", t=2)
                    elif name == "FR":
                        dst, src = hr[:].rearrange("p t n -> p (t n)"), ba[b][:]
                    else:
                        dst = h0[:, s, int(name[1]), :]
                        src = ba[b][:]
                    nc.scalar.copy(dst, src).then_inc(act_emptied, 1)

            act.wait_ge(zeroed, 2)
            act.wait_ge(small_loaded, 16 * 5)
            act.wait_ge(prep_done, 5)
            place_g(0)
            window(0, True)
            with act.Fori(1, WINDOWS - 1) as w:
                window(w, True)
            window(WINDOWS - 1, False)

        @block.vector
        def _(dve):
            dve.wait_ge(zeroed, 2)
            dve.wait_ge(prep_pe, 1)
            nc.vector.tensor_copy(w_t[:].rearrange("a k d -> a (k d)"), ba[0][:, 0:3 * D]).then_inc(prep_done, 1)
            dve.wait_ge(prep_pe, 2)
            nc.vector.tensor_scalar(m_score[:], ba[1][0:D, 0:D].rearrange("p (o d) -> p o d", o=1).broadcast_to([D, 2, D]),
                                    1.0 / SCALE, None, ALU.mult)
            nc.vector.tensor_copy(m_out[:], ba[1][0:D, D:2 * D]).then_inc(prep_done, 1)
            for q in range(4):
                dve.wait_ge(prep_pe, 3 + q)
                op = nc.vector.tensor_copy(tgt_t[:, q * 512:(q + 1) * 512], (ba + bd)[q][0:D, :])
            op.then_inc(prep_done, 1)
            for q in range(3):
                dve.wait_ge(prep_pe, 7 + q)
                op = nc.vector.tensor_copy(g_all[:, q * 512:(q + 1) * 512], (ba + bd)[q][:])
            op.then_inc(prep_done, 1)
            dve.wait_ge(prep_pe, 10)
            nc.vector.memset(dg[:, WINDOWS], 0.0)
            nc.vector.tensor_copy(dg[:, 0:WINDOWS].rearrange("p (k r) d -> p k r d", k=DIRECT),
                                  bd[1][:, 0:DIRECT * D].rearrange("p (k o d) -> p k o d", k=DIRECT, o=1)
                                  .broadcast_to([P, DIRECT, WINDOWS // DIRECT, D])).then_inc(prep_done, 1)
            dve.wait_ge(dmask_loaded, 16)
            dve.wait_ge(prep_done, 5)
            for b in range(2):
                nc.vector.tensor_copy(dg_now[:, b], dg[:, 0, :]).then_inc(dg_set, 1)

            def weigh(w, s):
                n, b = w * STEPS + s, s % 2
                dve.wait_ge(by_g_done, n + 1)
                if s >= 2 and not (isinstance(w, int) and w == WINDOWS - 1):
                    g = dg[:, w + 1, :] if isinstance(w, int) else dg[:, bass.ds(w + 1, 1), :].rearrange("p o d -> p (o d)")
                    nc.vector.tensor_scalar(dg_now[:, b], g, 1.0, None, ALU.mult).then_inc(dg_set, 1)
                nc.vector.tensor_reduce(dscore[:], by_g[:, b], AX_X, ALU.add).then_inc(dscored, 1)
                dve.wait_ge(dscored, n + 1)
                m = dmask[:, w, s * CHUNK:(s + 1) * CHUNK] if isinstance(w, int) else \
                    dmask[:, bass.ds(w, 1), s * CHUNK:(s + 1) * CHUNK].rearrange("p o l -> p (o l)")
                nc.vector.tensor_tensor(dmasked[:], dscore[:], m, ALU.mult).then_inc(dmasked_done, 1)
                dve.wait_ge(dmasked_done, n + 1)
                ge(dve, by_a_done, n - 1)
                nc.vector.tensor_scalar(datt[:, b], dmasked[:], 0.0, None, ALU.max).then_inc(datt_done, 1)

            def add_up(w, s):
                n, b = w * STEPS + s, s % 2
                dve.wait_ge(by_a_done, n + 1)
                dst = parts[:, w, s, :] if isinstance(w, int) else parts[:, bass.ds(w, 1), s, :].rearrange("p o d -> p (o d)")
                nc.vector.tensor_reduce(dst, by_a[:, b].rearrange("p l d -> p d l"), AX_X, ALU.add).then_inc(part_done, 1)

            def weigh_before(w, s):
                if not isinstance(w, int) or w > 0:
                    weigh(w - 1, s)

            def add_up_before(w, s):
                if s > 0 and (not isinstance(w, int) or w > 0):
                    add_up(w - 1, s - 1)
                elif not isinstance(w, int) or w > 1:
                    add_up(w - 2, STEPS - 1)

            def window(w, sums):
                base, fills = w * DVE_N, DVE_FILLS

                def empty(name, s):
                    i = index(fills, name, s)
                    b = fills[i][2]
                    dve.wait_ge(dve_filled, base + i + 1)
                    if name == "F5":
                        op = nc.vector.tensor_copy(h1[:, 2:4, s, :], bd[b][:].rearrange("p (t n) -> p t n", t=2))
                    elif name == "CT":
                        op = nc.vector.tensor_copy(csum_t[:], bd[b][0:D, 0:P])
                    op.then_inc(dve_emptied, 1)

                for s in range(STEPS - 1):
                    weigh_before(w, s)
                    if s == STEPS - 2 and sums:
                        pick(w)
                        empty("F5", s)
                    else:
                        add_up_before(w, s)
                        empty("F5", s)
                s = STEPS - 1
                dve.wait_ge(scored, w + 1)
                dve.wait_ge(msk_placed, w + 1)
                nc.vector.tensor_tensor(masked[:], ps_score[:, 0:2 * L], msk_own[:], ALU.mult).then_inc(masked_done, 1)
                dve.wait_ge(masked_done, w + 1)
                for k, (cut, n) in enumerate(CUTS):
                    a, b = (masked[:, cut + i * n:cut + (i + 1) * n].rearrange("p (o l) -> p o l", o=1).broadcast_to([P, P // n, n])
                            for i in range(2))
                    op = nc.vector.tensor_tensor(att[:, k * P:(k + 1) * P].rearrange("p (o l) -> p o l", l=n), a, b, ALU.add)
                op.then_inc(att_ready, 1)
                empty("CT", s)
                if sums:
                    add_up_before(w, s - 1)
                dve.wait_ge(at_done, w + 1)
                flat = w0[:].rearrange("p t s c -> p t (s c)")
                dst = bass.AP(flat.tensor, flat.offset, [flat.ap[0], [STEPS * COLS, TILES], [COLS + 8, STEPS], [1, 8]])
                nc.vector.tensor_scalar(dst, ps_at[:, 0:P].rearrange("p (t s k) -> p t s k", t=TILES, s=STEPS),
                                        0.0, None, ALU.max)
                for sp_ in range(2):
                    nc.vector.scalar_tensor_tensor(
                        out=w1[:, sp_], in0=ps_at[:, P:2 * P].rearrange("p (t c) -> p t c", t=TILES), scalar=0.0,
                        in1=const[:, C_SEL1 + sp_ * COLS:C_SEL1 + (sp_ + 1) * COLS].rearrange("p (o c) -> p o c", o=1).broadcast_to([P, TILES, COLS]),
                        op0=ALU.max, op1=ALU.mult)
                nc.vector.scalar_tensor_tensor(
                    out=wr[:], in0=ps_at[:, 2 * P:3 * P].rearrange("p (t c) -> p t c", t=TILES), scalar=0.0,
                    in1=const[:, C_SELR:C_SELR + COLS].rearrange("p (o c) -> p o c", o=1).broadcast_to([P, TILES, COLS]),
                    op0=ALU.max, op1=ALU.mult).then_inc(weights_placed, 1)
                weigh_before(w, s)
                empty("F5", s)
                finish(w, base + index(fills, "OUT", s) + 1)
                add_up_before(w, s)

            def pick(w):
                dve.wait_ge(ctx_done, w)
                for at, n, ps, c in ((0, 8, ps_c0[:], C_SELC), (8, 8, ps_c1[:], C_SELD), (16, 2, ps_cr, C_SELE)):
                    r = nc.vector.tensor_tensor(picked[:, at:at + n, :], ps.rearrange("p (k d) -> p k d", d=D),
                                                const[:, c:c + n].rearrange("p (k o) -> p k o", o=1).broadcast_to([P, n, D]),
                                                ALU.mult)
                    r.then_inc(ctx_read, 1)
                dve.wait_ge(ctx_read, w * 3)
                nc.vector.tensor_reduce(csum[:, 0:D], picked[:].rearrange("p k d -> p d k"), AX_X, ALU.add).then_inc(csum_ready, 1)

            def finish(w, filled):
                dve.wait_ge(dve_filled, filled)
                if isinstance(w, int) and w == 0:
                    nc.vector.tensor_copy(picked[:, 0, :], bd[1][:, 0:D]).then_inc(dve_emptied, 1)
                    return
                last = w - 1
                t = tgt[:, last, :] if isinstance(last, int) else tgt[:, bass.ds(last, 1), :].rearrange("p o d -> p (o d)")
                op = nc.vector.tensor_tensor(t, bd[1][:, 0:D], t, ALU.add)
                op.then_inc(dve_emptied, 1)

            nc.vector.memset(csum[:], 0.0).then_inc(csum_ready, 1)
            window(0, False)
            window(1, True)
            with dve.Fori(2, WINDOWS) as w:
                window(w, True)
            add_up(WINDOWS - 2, STEPS - 1)
            weigh(WINDOWS - 1, 0)
            weigh(WINDOWS - 1, 1)
            add_up(WINDOWS - 1, 0)
            pick(WINDOWS)
            weigh(WINDOWS - 1, 2)
            n = WINDOWS * DVE_N
            dve.wait_ge(dve_filled, n + 1)
            nc.vector.tensor_copy(csum_t[:], bd[1][0:D, 0:P]).then_inc(dve_emptied, 1)
            finish(WINDOWS, n + 2)
            add_up(WINDOWS - 1, 1)
            weigh(WINDOWS - 1, 3)
            add_up(WINDOWS - 1, 2)
            add_up(WINDOWS - 1, 3)
            dve.wait_ge(part_done, CHUNKS)
            for k in range(DIRECT):
                span = WINDOWS // DIRECT
                nc.vector.tensor_reduce(dsum[:, k, :], parts[:, k * span:(k + 1) * span].rearrange("p w s d -> p d (w s)"),
                                        AX_X, ALU.add).then_inc(dsum_done, 1)
            dve.wait_ge(dve_filled, n + 3)
            nc.vector.tensor_copy(dsum_t[:].rearrange("p k n -> p (k n)"), bd[0][0:D, :]).then_inc(dve_emptied, 1)
            dve.wait_ge(dve_filled, n + 4)
            nc.vector.tensor_tensor(tgt[:, WINDOWS:BLOCKS, :], bd[1][:, 0:DIRECT * D].rearrange("p (k d) -> p k d", d=D),
                                    tgt[:, WINDOWS:BLOCKS, :], ALU.add).then_inc(dve_emptied, 1)

        @block.tensor
        def _(pe):
            pe.wait_ge(small_loaded, 16 * 5)
            for k, m in enumerate((wq_s, wk_s, wv_s)):
                r = nc.tensor.transpose(ba[0][:, k * D:(k + 1) * D], m[:], ident[0:D, 0:D])
            r.then_inc(prep_pe, 1)
            pe.wait_ge(prep_done, 1)
            nc.tensor.matmul(ba[1][0:D, 0:D], w_t[:, 0, :], w_t[:, 1, :], start=True, stop=True)
            nc.tensor.matmul(ba[1][0:D, D:2 * D], w_t[:, 2, :], wo_s[:], start=True, stop=True).then_inc(prep_pe, 1)
            pe.wait_ge(prep_done, 2)
            pe.wait_ge(tgt_loaded, 16)
            for q in range(4):
                for j in range(4):
                    r = nc.tensor.transpose((ba + bd)[q][0:D, j * P:(j + 1) * P], tgt[:, q * 4 + j, :], ident)
                r.then_inc(prep_pe, 1)
            pe.wait_ge(prep_done, 3)
            for q in range(3):
                nc.tensor.matmul((ba + bd)[q][:], m_score[:].rearrange("p o d -> p (o d)"),
                                 tgt_t[:, q * 512:(q + 1) * 512], start=True, stop=True).then_inc(prep_pe, 1)

            for k in range(DIRECT):
                rows = (WINDOWS + k) * P
                op = nc.tensor.matmul(bd[1][:, k * D:(k + 1) * D], tgt_t[:, rows:rows + P], m_score[:, 0, :], start=True, stop=True)
            op.then_inc(prep_pe, 1)

            def score(w, s, q):
                if q == 0:
                    for half in range(2):
                        pe.wait_ge(loaded[s][half], (w + 1) * 16)
                if s == 0 and q == 0:
                    pe.wait_ge(g_placed, w + 1)
                    ge(pe, masked_done, w)
                for t in range(TILES):
                    r = nc.tensor.matmul(ps_score[t * COLS:(t + 1) * COLS, 0:2 * L], g_cols[:, t, s, q, :],
                                         hist[:, s, t, q, :],
                                         start=(s == 0 and q == 0), stop=(s == STEPS - 1 and q == 1),
                                         tile_position=(0, t * COLS))
                if s == STEPS - 1 and q == 1:
                    r.then_inc(scored, 1)

            def sum0(w, s):
                pe.wait_ge(act_emptied, (w - 1) * ACT_N + index(ACT_FILLS, "F3", s) + 1)
                for t in range(TILES):
                    nc.tensor.matmul(ps_c0[t * COLS:(t + 1) * COLS, :], w0[:, t, s, :], h0[:, s, t, :],
                                     start=(s == 0), stop=(s == STEPS - 1), tile_position=(0, t * COLS))

            def sum1(w, j):
                pe.wait_ge(act_emptied, (w - 1) * ACT_N + index(ACT_FILLS, "F4", 2 * j + 1) + 1)
                pe.wait_ge(dve_emptied, (w - 1) * DVE_N + index(DVE_FILLS, "F5", 2 * j + 1) + 1)
                for t in range(TILES):
                    nc.tensor.matmul(ps_c1[t * COLS:(t + 1) * COLS, :], w1[:, j, t, :],
                                     h1[:, t, 2 * j:2 * j + 2, :].rearrange("p s n -> p (s n)"),
                                     start=(j == 0), stop=(j == 1), tile_position=(0, t * COLS))

            def sum_rest(w):
                pe.wait_ge(act_emptied, w * ACT_N)
                for t in range(TILES):
                    r = nc.tensor.matmul(ps_cr[t * COLS:(t + 1) * COLS, :], wr[:, t, :], hr[:, t, :],
                                         start=True, stop=True, tile_position=(0, t * COLS))
                r.then_inc(ctx_done, 1)

            def before_sums(w):
                pe.wait_ge(weights_placed, w)
                ge(pe, ctx_read, (w - 1) * 3)

            def free(w, fills, n, emptied, banks, name, s):
                i = index(fills, name, s)
                b = fills[i][2]
                last = max(k for k in range(-n, i) if fills[k % n][2] == b)
                ge(pe, emptied, w * n + last + 1)
                return banks[b]

            def act_bank(w, name, s):
                return free(w, ACT_FILLS, ACT_N, act_emptied, ba, name, s)

            def dve_bank(w, name, s):
                return free(w, DVE_FILLS, DVE_N, dve_emptied, bd, name, s)

            def turn0(w, s, t):
                ps = act_bank(w, f"F{t}", s)
                for r in range(PAIRS):
                    op = nc.tensor.transpose(ps[:, r * P:(r + 1) * P], hist[:, s, t, r // 2, r % 2 * L0:(r % 2 + 1) * L0], ident)
                op.then_inc(act_filled, 1)

            def turn1(w, s, half):
                if not half:
                    pe.wait_ge(rest_copied, w * STEPS + s + 1)
                ps = dve_bank(w, "F5", s) if half else act_bank(w, "F4", s)
                for k in range(4):
                    t, c = 2 * half + k // 2, k % 2
                    op = nc.tensor.transpose(ps[:, k * P:(k + 1) * P], hist[:, s, t, c, 2 * L0:2 * (L0 + L1)], ident)
                op.then_inc(dve_filled if half else act_filled, 1)

            def turn_rest(w):
                pe.wait_ge(rest_copied, (w + 1) * STEPS)
                ps = act_bank(w, "FR", STEPS - 1)
                for t in range(TILES):
                    op = nc.tensor.transpose(ps[:, t * P:(t + 1) * P], rest[:, t, :, :].rearrange("p r l -> p (r l)"), ident)
                op.then_inc(act_filled, 1)

            def turn_weights(w):
                pe.wait_ge(att_ready, w + 1)
                ge(pe, ctx_read, w * 3)
                for k in range(len(CUTS)):
                    op = nc.tensor.transpose(ps_at[:, k * P:(k + 1) * P], att[:, k * P:(k + 1) * P], ident)
                op.then_inc(at_done, 1)

            def csum_turn(w, b):
                pe.wait_ge(csum_ready, w + 1)
                nc.tensor.transpose(b[:, 0:P], csum[:], ident).then_inc(dve_filled, 1)

            def out_product(b, emptied):
                pe.wait_ge(dve_emptied, emptied)
                nc.tensor.matmul(b[:, 0:D], csum_t[:], m_out[:], start=True, stop=True).then_inc(dve_filled, 1)

            def window(w, sums, more):
                for s in range(STEPS):
                    last = s == STEPS - 1
                    ahead = (lambda q: score(w, s + 1, q)) if not last else (lambda q: score(w + 1, 0, q))
                    if sums:
                        if s == 0:
                            before_sums(w)
                            sum0(w, 0)
                        elif s == 1:
                            sum0(w, 1)
                            sum0(w, 2)
                        elif s == 2:
                            sum1(w, 1)
                            sum_rest(w)
                    turn0(w, s, 0)
                    turn0(w, s, 1)
                    if sums:
                        if s == 0:
                            sum1(w, 0)
                        elif s == 1:
                            sum0(w, 3)
                    if last:
                        csum_turn(w, dve_bank(w, "CT", s))
                    turn1(w, s, 0)
                    turn0(w, s, 2)
                    if last:
                        turn_weights(w)
                    if more or not last:
                        ahead(0)
                    turn0(w, s, 3)
                    turn1(w, s, 1)
                    if last:
                        out_product(dve_bank(w, "OUT", s), w * DVE_N + index(DVE_FILLS, "CT", s) + 1)
                        turn_rest(w)
                    if more or not last:
                        ahead(1)

            pe.wait_ge(prep_done, 5)
            score(0, 0, 0)
            score(0, 0, 1)
            window(0, False, True)
            with pe.Fori(1, WINDOWS - 1) as w:
                window(w, True, True)
            window(WINDOWS - 1, True, False)
            w = WINDOWS
            before_sums(w)
            for s in range(STEPS):
                sum0(w, s)
            sum1(w, 0)
            sum1(w, 1)
            sum_rest(w)
            n = w * DVE_N
            csum_turn(w, bd[1])
            out_product(bd[1], n + 1)
            pe.wait_ge(dsum_done, DIRECT)
            for k in range(DIRECT):
                op = nc.tensor.transpose(bd[0][0:D, k * P:(k + 1) * P], dsum[:, k, :], ident)
            op.then_inc(dve_filled, 1)
            pe.wait_ge(dve_emptied, n + 3)
            for k in range(DIRECT):
                op = nc.tensor.matmul(bd[1][:, k * D:(k + 1) * D], dsum_t[:, k, :], m_out[:], start=True, stop=True)
            op.then_inc(dve_filled, 1)


def constants():
    import numpy as np
    c = np.zeros((P, C_END), np.float32)
    p = np.arange(P)
    c[:, C_ID:C_ID + P] = np.eye(P)
    b = p % COLS
    s, pr, par = b // 8, b // 2 % PAIRS, b % 2
    c[p, C_SELS + pr % 2] = 1
    c[p, C_SELC + pr * 2 + par] = 1
    c[p, C_SELD + (s % 2) * 4 + (pr // 2) * 2 + par] = 1
    c[p, C_SELE + par] = 1
    col = np.arange(COLS)
    for j in range(2):
        c[:, C_SEL1 + j * COLS:C_SEL1 + (j + 1) * COLS] = (col // 16 == j) & (col // 2 % 2 == (p // L1)[:, None])
    c[:, C_SELR:C_SELR + COLS] = col // 2 == (p // LR)[:, None]
    return c


def kernel(**inputs):
    import numpy as np
    import concourse.bacc as bacc
    from concourse.bass_utils import run_bass_kernel_spmd

    nc = bacc.Bacc("TRN2", target_bir_lowering=False, num_devices=1)
    history = np.asarray(inputs["r_history_sequence"])
    hist = history[:WINDOWS * P].reshape(WINDOWS, TILES, STEPS, 2, 2, PAR, L, D)
    hist = hist.transpose(0, 2, 5, 7, 1, 3, 4, 6)
    laid, at = [], 0
    for _, n in CUTS:
        laid.append(hist[..., at:at + n].reshape(WINDOWS * STEPS, P, TILES, 2, 2 * n))
        at += n
    hist = np.concatenate(laid, axis=-1).reshape(WINDOWS * STEPS, P, 2, TILES * 2 * L)
    hist = np.ascontiguousarray(hist.transpose(0, 2, 1, 3))
    direct = np.zeros((DIRECT, P, BLOCK_CHUNKS * CHUNK, D), history.dtype)
    direct[:, :, :L] = history[WINDOWS * P:].reshape(DIRECT, P, L, D)
    direct = direct.reshape(DIRECT, P, BLOCK_CHUNKS, CHUNK * D).transpose(0, 2, 1, 3)
    mask = np.asarray(inputs["r_mask"]).reshape(B, L)
    direct_mask = np.zeros((DIRECT, P, BLOCK_CHUNKS * CHUNK), mask.dtype)
    direct_mask[:, :, :L] = mask[WINDOWS * P:].reshape(DIRECT, P, L)
    direct_mask = direct_mask.transpose(1, 0, 2).reshape(P, WINDOWS, STEPS * CHUNK)
    arrays = {
        "target": np.ascontiguousarray(inputs["r_target_item"]),
        "history": hist,
        "direct": np.ascontiguousarray(direct).reshape(CHUNKS, P, CHUNK * D),
        "mask": np.ascontiguousarray(mask),
        "direct_mask": np.ascontiguousarray(direct_mask),
        "wq": np.ascontiguousarray(inputs["L0_rec_W_q"]),
        "wk": np.ascontiguousarray(inputs["L0_rec_W_k"]),
        "wv": np.ascontiguousarray(inputs["L0_rec_W_v"]),
        "wo": np.ascontiguousarray(inputs["L0_rec_W_o"]),
        "consts": constants(),
    }
    args = [nc.dram_tensor(n, a.shape, mybir.dt.from_np(a.dtype), kind="ExternalInput").ap() for n, a in arrays.items()]
    out = nc.dram_tensor("out", (B, D), F32, kind="ExternalOutput").ap()
    attention_kernel(nc, *args, out)
    r = run_bass_kernel_spmd(nc, [arrays], core_ids=[0])
    return r.results[0]["out"]
```

```python
from contextlib import ExitStack

import concourse.bass as bass
from concourse import mybir

F32 = mybir.dt.float32
I32 = mybir.dt.int32
ALU = mybir.AluOpType
ACT = mybir.ActivationFunctionType
AX_X = mybir.AxisListType.X

P = 128
B, L, D, A = 2048, 200, 64, 128
SCALE = float(A) ** 0.5
BLOCKS = B // P
DIRECT = BLOCKS // 4
WINDOWS = BLOCKS - DIRECT
TILES, STEPS, PAIRS, PAR = 4, 4, 4, 2
TP = STEPS * PAIRS
L0, L1, LR = 128, 64, 8
COLS = P // TILES
CHUNKS = WINDOWS * STEPS
BLOCK_CHUNKS = CHUNKS // DIRECT
BESIDE = -(-L * DIRECT // WINDOWS)
SIZES = [-(-(BESIDE - s) // STEPS) for s in range(STEPS)]
STARTS = [sum(SIZES[:s]) for s in range(STEPS)]
CHUNK = max(SIZES)
BLOCK_WINDOWS = WINDOWS // DIRECT
assert sum(SIZES) == BESIDE and BESIDE * BLOCK_WINDOWS >= L
LOAD_BEHIND = 1
WEIGH_BEHIND = 1
CUTS = ((0, L0), (2 * L0, L1), (2 * (L0 + L1), LR))

C_ID, C_SELS, C_SELC, C_SELD, C_SELE, C_SEL1, C_SELR, C_END = 0, 128, 130, 138, 146, 148, 212, 244

ACT_ORDER = [(f"F{f}", s) for s in range(STEPS) for f in (0, 1, 4, 2, 3)] + [("FR", STEPS - 1)]
ACT_FILLS = [(name, s, k % 2) for k, (name, s) in enumerate(ACT_ORDER)]
DVE_FILLS = [("F5", 0, 0), ("F5", 1, 1), ("F5", 2, 0), ("F5", 3, 0), ("CT", 3, 1), ("OUT", 3, 1)]
EARLY_F5 = 2
ACT_N, DVE_N = len(ACT_FILLS), len(DVE_FILLS)


def attention_kernel(nc, target_t, history, direct, mask, direct_mask, weights, consts, out):
    with ExitStack() as ctx:
        def sb(name, shape, dt=F32):
            return ctx.enter_context(nc.sbuf_tensor(name, shape, dt))

        def bank(name):
            return ctx.enter_context(nc.psum_tensor(name, [P, 512], F32))

        def sem(name):
            return ctx.enter_context(nc.semaphore(name))

        hist = sb("hist", [P, STEPS, TILES, 2, 2 * L])
        h0 = sb("h0", [P, STEPS, TILES, PAIRS * P])
        h1 = sb("h1", [P, TILES, STEPS, 2 * P])
        hr = sb("hr", [P, TILES, P])
        rest = sb("rest", [P, TILES, TP, LR])
        g_all = sb("g_all", [P, WINDOWS * P])
        g_cols = sb("g_cols", [P, TILES, STEPS, 2, COLS])
        outs = sb("outs", [P, BLOCKS, D])
        tgt_t = sb("tgt_t", [D, B])
        msk = sb("msk", [P, L], I32)
        const = sb("const", [P, C_END])
        w0 = sb("w0", [P, TILES, STEPS, COLS])
        w1 = sb("w1", [P, 2, TILES, COLS])
        wr = sb("wr", [P, TILES, COLS])
        msk_own = sb("msk_own", [P, 2 * L])
        masked = sb("masked", [P, 2 * L])
        att = sb("att", [P, 3 * P])
        picked = sb("picked", [P, 18, D])
        csum = sb("csum", [P, P])
        csum_t = sb("csum_t", [2 * D, P])
        dhist = sb("dhist", [P, STEPS, CHUNK, D])
        dmask = sb("dmask", [P, WINDOWS, BESIDE], I32)
        dg = sb("dg", [P, WINDOWS + 1, D])
        dg_now = sb("dg_now", [P, 2, D])
        by_g = sb("by_g", [P, 2, CHUNK, D])
        by_a = sb("by_a", [P, 2, CHUNK, D])
        dscore = sb("dscore", [P, CHUNK])
        dmasked = sb("dmasked", [P, CHUNK])
        datt = sb("datt", [P, 2, CHUNK])
        parts = sb("parts", [P, WINDOWS, STEPS, D])
        dsum = sb("dsum", [P, DIRECT, D])
        dsum_t = sb("dsum_t", [2 * D, DIRECT, P])
        w_s = sb("w_s", [A, 4, D])
        warm = sb("warm", [P, 1])
        m_score = sb("m_score", [D, 2, D])
        m_out = sb("m_out", [2 * D, D])

        ps_score, ps_c0, ps_c1, ps_misc = bank("ps_score"), bank("ps_c0"), bank("ps_c1"), bank("ps_misc")
        ba = [bank("ba0"), bank("ba1")]
        bd = [bank("bd0"), bank("bd1")]
        ps_at = ps_misc[:, 0:3 * P]
        ps_cr = ps_misc[:, 3 * P:4 * P]

        ident = const[:, C_ID:C_ID + P]

        loaded = [[sem(f"hist_loaded{s}{half}") for half in range(2)] for s in range(STEPS)]
        weights_loaded, tgt_t_loaded, const_loaded = sem("weights_loaded"), sem("tgt_t_loaded"), sem("const_loaded")
        msk_loaded, tgt_placed = sem("msk_loaded"), sem("tgt_placed")
        out_stored = sem("out_stored")
        zeroed = sem("zeroed")
        prep_pe, prep_done = sem("prep_pe"), sem("prep_done")
        g_placed = sem("g_placed")
        rest_copied = sem("rest_copied")
        scored = sem("scored")
        msk_placed, masked_done, att_ready = sem("msk_placed"), sem("masked_done"), sem("att_ready")
        at_done = sem("at_done")
        weights_placed = sem("weights_placed")
        ctx_done, ctx_read = sem("ctx_done"), sem("ctx_read")
        csum_ready = sem("csum_ready")
        dloaded = [sem(f"direct_loaded{s}") for s in range(STEPS)]
        dmask_loaded, dg_set = sem("dmask_loaded"), sem("dg_set")
        by_g_done, dscored, dmasked_done, datt_done = sem("by_g_done"), sem("dscored"), sem("dmasked_done"), sem("datt_done")
        by_a_done, part_done, dsum_done = sem("by_a_done"), sem("part_done"), sem("dsum_done")
        ctx_late_done = sem("ctx_late_done")
        dsum_turned, dsum_copied, dproduct_done = sem("dsum_turned"), sem("dsum_copied"), sem("dproduct_done")
        direct_done, window_done = sem("direct_done"), sem("window_done")
        act_filled, act_emptied = sem("act_filled"), sem("act_emptied")
        dve_filled, dve_emptied = sem("dve_filled"), sem("dve_emptied")

        def index(fills, name, s):
            return next(i for i, x in enumerate(fills) if x[0] == name and x[1] == s)

        def back(w, s, n):
            if s < n:
                w, s = w - 1, s + STEPS
            return None if isinstance(w, int) and w < 0 else (w, s - n)

        def ge(eng, s, value):
            if not isinstance(value, int) or value > 0:
                eng.wait_ge(s, value)

        block = ctx.enter_context(nc.Block())

        @block.sync
        def _(sp):
            def value(x):
                return x if isinstance(x, int) else sp.snap(x)

            def load(block, s, half):
                sp.dma_start(hist[:, s, 2 * half:2 * half + 2].rearrange("p t q l -> p (t q l)"),
                             history[bass.ds(block, 1), half].rearrange("o p n -> (o p) n")).then_inc(loaded[s][half], 16)

            def load_direct(w, s):
                sp.dma_start(dhist[:, s, 0:SIZES[s]].rearrange("p l d -> p (l d)"),
                             direct[bass.ds(w, 1), :, STARTS[s] * D:(STARTS[s] + SIZES[s]) * D].rearrange("o p n -> (o p) n")).then_inc(dloaded[s], 16)

            def load_mask(row):
                sp.dma_start(msk[:], mask[bass.ds(row, P), :]).then_inc(msk_loaded, 16)

            def store(first, end):
                sp.dma_start(out[:, first * D:end * D], outs[:, first:end].rearrange("p w d -> p (w d)")).then_inc(out_stored, 16)

            def window(w):
                last = w - 1
                for s in range(STEPS):
                    if s == STEPS - 1:
                        row, placed = value(w * P), value(w)
                        sp.wait_ge(msk_placed, placed)
                        load_mask(row)
                    block = value(w * STEPS + s)
                    filled = value(last * ACT_N + index(ACT_FILLS, "F4", s) + 1)
                    sp.wait_ge(act_filled, filled)
                    load(block, s, 0)
                    if s < EARLY_F5:
                        filled = value(last * DVE_N + index(DVE_FILLS, "F5", s) + 1)
                        sp.wait_ge(dve_filled, filled)
                    else:
                        filled = value(last * ACT_N + index(ACT_FILLS, "F3", s) + 1)
                        sp.wait_ge(act_filled, filled)
                    load(block, s, 1)
                    direct_beside(w, s)

            def direct_beside(w, s):
                if back(w, s, LOAD_BEHIND) is None:
                    return
                w, s = back(w, s, LOAD_BEHIND)
                w_value = value(w)
                if not isinstance(w, int) or w > 0:
                    taken = value((w - 1) * STEPS + s + 1)
                    sp.wait_ge(by_a_done, taken)
                load_direct(w_value, s)

            sp.dma_start(w_s[:].rearrange("a k d -> a (k d)"), weights).then_inc(weights_loaded, 16)
            sp.dma_start(tgt_t[:], target_t).then_inc(tgt_t_loaded, 16)
            sp.dma_start(const[:], consts).then_inc(const_loaded, 16)
            for s in range(STEPS):
                load(s, s, 0)
                load(s, s, 1)
                direct_beside(0, s)
                if s == LOAD_BEHIND:
                    load_mask(0)
                    sp.dma_start(dmask[:].rearrange("p w l -> p (w l)"), direct_mask).then_inc(dmask_loaded, 16)
            window(1)
            with sp.Fori(2, WINDOWS) as w:
                window(w)
            for s in range(LOAD_BEHIND):
                direct_beside(WINDOWS, s)
            sp.wait_ge(dve_emptied, (WINDOWS - 1) * DVE_N + index(DVE_FILLS, "OUT", STEPS - 1) + 1)
            store(0, WINDOWS - 1)
            sp.wait_ge(direct_done, 1)
            store(WINDOWS, BLOCKS)
            sp.wait_ge(window_done, 1)
            store(WINDOWS - 1, WINDOWS)
            sp.wait_ge(out_stored, 16 * 3)

        @block.gpsimd
        def _(pool):
            nc.gpsimd.memset(g_cols[:], 0.0).then_inc(zeroed, 1)
            nc.gpsimd.memset(w0[:], 0.0).then_inc(zeroed, 1)

            def times_g(w, s):
                n, b, size = w * STEPS + s, s % 2, SIZES[s]
                pool.wait_ge(dloaded[s], (w + 1) * 16)
                ge(pool, dscored, n - 1)
                pool.wait_ge(dg_set, w * 2 + b + 1)
                nc.gpsimd.tensor_tensor(by_g[:, b, 0:size], dhist[:, s, 0:size],
                                        dg_now[:, b].rearrange("p (o d) -> p o d", o=1).broadcast_to([P, size, D]),
                                        ALU.mult).then_inc(by_g_done, 1)

            def times_a(w, s):
                n, b, size = w * STEPS + s, s % 2, SIZES[s]
                pool.wait_ge(datt_done, n + 1)
                dst = by_a[:, b, 0:size]
                if isinstance(w, int) and n == CHUNKS - 1:
                    dst = by_g[:, b, 0:size]
                else:
                    ge(pool, part_done, n - 1)
                nc.gpsimd.tensor_tensor(dst, dhist[:, s, 0:size],
                                        datt[:, b, 0:size].rearrange("p (l o) -> p l o", o=1).broadcast_to([P, size, D]),
                                        ALU.mult).then_inc(by_a_done, 1)

            for s in range(STEPS):
                times_g(0, s)
                if s > 0:
                    times_a(0, s - 1)
            with pool.Fori(1, WINDOWS) as w:
                for s in range(STEPS):
                    times_g(w, s)
                    if s > 0:
                        times_a(w, s - 1)
                    else:
                        times_a(w - 1, STEPS - 1)
            times_a(WINDOWS - 1, STEPS - 1)

        @block.scalar
        def _(act):
            def place_g(w, first, end):
                us = slice(2 * first, 2 * end)
                for par in range(PAR):
                    rows = slice(par * D, (par + 1) * D)
                    if isinstance(w, int):
                        src = g_all[rows, w * P:(w + 1) * P]
                    else:
                        src = g_all[rows, bass.ds(w * P, P)]
                    src = src.rearrange("p (t u i r) -> p t u i r", t=TILES, u=STEPS * 2, i=2)[:, :, us, :, par]
                    flat = g_cols[rows].rearrange("p t s q c -> p t (s q c)")
                    dst = bass.AP(flat.tensor, flat.offset + par + us.start * (COLS + 4),
                                  [flat.ap[0], [STEPS * 2 * COLS, TILES], [COLS + 4, us.stop - us.start], [2, 2]])
                    last = nc.scalar.copy(dst, src)
                last.then_inc(g_placed, 1)

            def place_target(w):
                src = tgt_t[:, w * P:(w + 1) * P] if isinstance(w, int) else tgt_t[:, bass.ds(w * P, P)]
                nc.scalar.copy(csum_t[D:2 * D, :], src).then_inc(tgt_placed, 1)

            def place_mask(w):
                act.wait_ge(msk_loaded, (w + 1) * 16)
                ge(act, masked_done, w)
                at = 0
                for cut, n in CUTS:
                    for i in range(2):
                        last = nc.scalar.activation(msk_own[:, cut + i * n:cut + (i + 1) * n], msk[:, at:at + n], ACT.Copy,
                                                    scale=const[:, C_SELS + i:C_SELS + i + 1])
                    at += n
                last.then_inc(msk_placed, 1)

            def copy_rest(w, s):
                for half in range(2):
                    act.wait_ge(loaded[s][half], (w + 1) * 16)
                if s == 0:
                    ge(act, act_filled, w * ACT_N)
                nc.scalar.copy(rest[:, :, s * PAIRS:(s + 1) * PAIRS, :].rearrange("p t (q i) l -> p t q (i l)", i=2),
                               hist[:, s, :, :, 2 * (L0 + L1):2 * L]).then_inc(rest_copied, 1)

            def window(w, more):
                k = 0
                for name, s, b in ACT_FILLS:
                    k += 1
                    act.wait_ge(act_filled, w * ACT_N + k)
                    if name == "F4":
                        dst = h1[:, 0:2, s, :]
                        src = ba[b][:].rearrange("p (t n) -> p t n", t=2)
                    elif name == "FR":
                        dst, src = hr[:].rearrange("p t n -> p (t n)"), ba[b][:]
                    else:
                        dst = h0[:, s, int(name[1]), :]
                        src = ba[b][:]
                    nc.scalar.copy(dst, src).then_inc(act_emptied, 1)
                    if name == "F3" and s < STEPS - 1:
                        copy_rest(w, s + 1)
                    if name == "F3" and s == 1:
                        place_mask(w)
                    if name == "F3" and s == 2 and more:
                        place_g(w + 1, 0, 2)
                    if name == "FR":
                        place_target(w)
                    if name == "FR" and more:
                        copy_rest(w + 1, 0)
                        place_g(w + 1, 2, STEPS)

            act.wait_ge(zeroed, 2)
            nc.scalar.copy(warm[:], w0[:, 0, 0, 0:1])
            act.wait_ge(tgt_t_loaded, 16)
            nc.scalar.copy(dsum_t[D:2 * D].rearrange("p k n -> p (k n)"), tgt_t[:, WINDOWS * P:B])
            place_target(0)
            act.wait_ge(prep_done, 2)
            place_g(0, 0, 2)
            place_g(0, 2, STEPS)
            act.wait_ge(const_loaded, 16)
            nc.scalar.copy(m_out[D:2 * D, :], const[D:2 * D, C_ID + D:C_ID + 2 * D])
            act.wait_ge(prep_done, 5)
            copy_rest(0, 0)
            window(0, True)
            with act.Fori(1, WINDOWS - 1) as w:
                window(w, True)
            window(WINDOWS - 1, False)
            act.wait_ge(csum_ready, WINDOWS)
            act.wait_ge(ctx_late_done, 1)
            for k in range(8):
                op = nc.scalar.activation(picked[:, 8 + k, :], ps_c1[:, k * D:(k + 1) * D], ACT.Copy,
                                          scale=const[:, C_SELD + k:C_SELD + k + 1])
            op.then_inc(ctx_read, 1)
            act.wait_ge(ctx_late_done, 2)
            for k in range(2):
                op = nc.scalar.activation(picked[:, 16 + k, :], ps_cr[:, k * D:(k + 1) * D], ACT.Copy,
                                          scale=const[:, C_SELE + k:C_SELE + k + 1])
            op.then_inc(ctx_read, 1)
            act.wait_ge(dsum_turned, 1)
            nc.scalar.copy(dsum_t[0:D].rearrange("p k n -> p (k n)"), bd[0][0:D, :]).then_inc(dsum_copied, 1)
            act.wait_ge(dproduct_done, 1)
            nc.scalar.copy(outs[:, WINDOWS:BLOCKS, :].rearrange("p k d -> p (k d)"), bd[1][:, 0:DIRECT * D]).then_inc(direct_done, 1)

        @block.vector
        def _(dve):
            dve.wait_ge(zeroed, 2)
            dve.wait_ge(prep_pe, 1)
            nc.vector.tensor_scalar(m_score[:], ba[1][0:D, 0:D].rearrange("p (o d) -> p o d", o=1).broadcast_to([D, 2, D]),
                                    1.0 / SCALE, None, ALU.mult)
            nc.vector.tensor_copy(m_out[0:D, :], ba[1][0:D, D:2 * D]).then_inc(prep_done, 1)
            dve.wait_ge(prep_pe, 2)
            nc.vector.tensor_copy(g_all[:, 0:512], ba[0][:]).then_inc(prep_done, 1)
            dve.wait_ge(prep_pe, 3)
            nc.vector.memset(dg[:, WINDOWS], 0.0)
            nc.vector.tensor_copy(dg[:, 0:WINDOWS].rearrange("p (k r) d -> p k r d", k=DIRECT),
                                  ba[1][:, P:P + DIRECT * D].rearrange("p (k o d) -> p k o d", k=DIRECT, o=1)
                                  .broadcast_to([P, DIRECT, WINDOWS // DIRECT, D])).then_inc(prep_done, 1)
            for q in (1, 2):
                dve.wait_ge(prep_pe, 3 + q)
                nc.vector.tensor_copy(g_all[:, q * 512:(q + 1) * 512], bd[q - 1][:]).then_inc(prep_done, 1)
            dve.wait_ge(prep_done, 3)
            for b in range(2):
                nc.vector.tensor_copy(dg_now[:, b], dg[:, 0, :]).then_inc(dg_set, 1)

            def weigh(w, s):
                n, b, size = w * STEPS + s, s % 2, SIZES[s]
                dve.wait_ge(by_g_done, n + 1)
                if isinstance(w, int) and n == 0:
                    dve.wait_ge(dmask_loaded, 16)
                if s >= 2 and not (isinstance(w, int) and w == WINDOWS - 1):
                    g = dg[:, w + 1, :] if isinstance(w, int) else dg[:, bass.ds(w + 1, 1), :].rearrange("p o d -> p (o d)")
                    nc.vector.tensor_scalar(dg_now[:, b], g, 1.0, None, ALU.mult).then_inc(dg_set, 1)
                nc.vector.tensor_reduce(dscore[:, 0:size], by_g[:, b, 0:size], AX_X, ALU.add).then_inc(dscored, 1)
                dve.wait_ge(dscored, n + 1)
                m = dmask[:, w, STARTS[s]:STARTS[s] + size] if isinstance(w, int) else \
                    dmask[:, bass.ds(w, 1), STARTS[s]:STARTS[s] + size].rearrange("p o l -> p (o l)")
                nc.vector.tensor_tensor(dmasked[:, 0:size], dscore[:, 0:size], m, ALU.mult).then_inc(dmasked_done, 1)
                dve.wait_ge(dmasked_done, n + 1)
                ge(dve, by_a_done, n - 1)
                nc.vector.tensor_scalar(datt[:, b, 0:size], dmasked[:, 0:size], 0.0, None, ALU.max).then_inc(datt_done, 1)

            def add_up(w, s):
                n, b = w * STEPS + s, s % 2
                dve.wait_ge(by_a_done, n + 1)
                dst = parts[:, w, s, :] if isinstance(w, int) else parts[:, bass.ds(w, 1), s, :].rearrange("p o d -> p (o d)")
                src = by_g if isinstance(w, int) and n == CHUNKS - 1 else by_a
                nc.vector.tensor_reduce(dst, src[:, b, 0:SIZES[s]].rearrange("p l d -> p d l"), AX_X, ALU.add).then_inc(part_done, 1)

            def weigh_behind(w, s):
                at = back(w, s, WEIGH_BEHIND)
                if at is not None:
                    weigh(*at)

            def add_up_behind(w, s):
                at = back(w, s, WEIGH_BEHIND + 1)
                if at is not None:
                    add_up(*at)

            def window(w, sums, final=False):
                base, fills = w * DVE_N, DVE_FILLS

                def empty(name, s):
                    i = index(fills, name, s)
                    b = fills[i][2]
                    dve.wait_ge(dve_filled, base + i + 1)
                    if name == "F5":
                        op = nc.vector.tensor_copy(h1[:, 2:4, s, :], bd[b][:].rearrange("p (t n) -> p t n", t=2))
                    elif name == "CT":
                        op = nc.vector.tensor_copy(csum_t[0:D, :], bd[b][0:D, 0:P])
                    op.then_inc(dve_emptied, 1)

                for s in range(STEPS - 1):
                    if final and s < 2:
                        for k in range(DIRECT - 1)[s::2]:
                            sum_block(k)
                    weigh_behind(w, s)
                    if s == STEPS - 2 and sums:
                        if final:
                            add_up_behind(w, s)
                        pick(w)
                        empty("F5", s)
                    else:
                        add_up_behind(w, s)
                        if final and s == 1:
                            dve.wait_ge(part_done, CHUNKS - STEPS)
                            nc.vector.tensor_reduce(dsum[:, DIRECT - 1, :], chunk_parts[:, :, (DIRECT - 1) * BLOCK_CHUNKS:CHUNKS - STEPS],
                                                    AX_X, ALU.add).then_inc(dsum_done, 1)
                        empty("F5", s)
                s = STEPS - 1
                dve.wait_ge(scored, w + 1)
                dve.wait_ge(msk_placed, w + 1)
                nc.vector.tensor_tensor(masked[:], ps_score[:, 0:2 * L], msk_own[:], ALU.mult).then_inc(masked_done, 1)
                dve.wait_ge(masked_done, w + 1)
                for k, (cut, n) in enumerate(CUTS):
                    a, b = (masked[:, cut + i * n:cut + (i + 1) * n].rearrange("p (o l) -> p o l", o=1).broadcast_to([P, P // n, n])
                            for i in range(2))
                    op = nc.vector.tensor_tensor(att[:, k * P:(k + 1) * P].rearrange("p (o l) -> p o l", l=n), a, b, ALU.add)
                op.then_inc(att_ready, 1)
                empty("F5", s)
                empty("CT", s)
                if sums and not final:
                    add_up_behind(w, s - 1)
                dve.wait_ge(at_done, w + 1)
                flat = w0[:].rearrange("p t s c -> p t (s c)")
                dst = bass.AP(flat.tensor, flat.offset, [flat.ap[0], [STEPS * COLS, TILES], [COLS + 8, STEPS], [1, 8]])
                nc.vector.tensor_scalar(dst, ps_at[:, 0:P].rearrange("p (t s k) -> p t s k", t=TILES, s=STEPS),
                                        0.0, None, ALU.max)
                for sp_ in range(2):
                    nc.vector.scalar_tensor_tensor(
                        out=w1[:, sp_], in0=ps_at[:, P:2 * P].rearrange("p (t c) -> p t c", t=TILES), scalar=0.0,
                        in1=const[:, C_SEL1 + sp_ * COLS:C_SEL1 + (sp_ + 1) * COLS].rearrange("p (o c) -> p o c", o=1).broadcast_to([P, TILES, COLS]),
                        op0=ALU.max, op1=ALU.mult)
                nc.vector.scalar_tensor_tensor(
                    out=wr[:], in0=ps_at[:, 2 * P:3 * P].rearrange("p (t c) -> p t c", t=TILES), scalar=0.0,
                    in1=const[:, C_SELR:C_SELR + COLS].rearrange("p (o c) -> p o c", o=1).broadcast_to([P, TILES, COLS]),
                    op0=ALU.max, op1=ALU.mult).then_inc(weights_placed, 1)
                weigh_behind(w, s)
                finish(w, base + index(fills, "OUT", s) + 1)
                if final:
                    weigh_behind(w + 1, 0)
                add_up_behind(w, s)

            def pick_part(part):
                at, n, ps, c = ((0, 8, ps_c0[:], C_SELC), (8, 8, ps_c1[:], C_SELD), (16, 2, ps_cr, C_SELE))[part]
                nc.vector.tensor_tensor(picked[:, at:at + n, :], ps.rearrange("p (k d) -> p k d", d=D),
                                        const[:, c:c + n].rearrange("p (k o) -> p k o", o=1).broadcast_to([P, n, D]),
                                        ALU.mult).then_inc(ctx_read, 1)

            chunk_parts = parts[:].rearrange("p w s d -> p d (w s)")

            def sum_block(k):
                dve.wait_ge(part_done, (k + 1) * BLOCK_CHUNKS)
                nc.vector.tensor_reduce(dsum[:, k, :], chunk_parts[:, :, k * BLOCK_CHUNKS:(k + 1) * BLOCK_CHUNKS],
                                        AX_X, ALU.add).then_inc(dsum_done, 1)

            def pick(w):
                dve.wait_ge(ctx_done, w)
                for part in range(3):
                    pick_part(part)
                dve.wait_ge(ctx_read, w * 3)
                nc.vector.tensor_reduce(csum[:, 0:D], picked[:].rearrange("p k d -> p d k"), AX_X, ALU.add).then_inc(csum_ready, 1)

            def finish(w, filled):
                dve.wait_ge(dve_filled, filled)
                if isinstance(w, int) and w == 0:
                    nc.vector.tensor_copy(picked[:, 0, :], bd[1][:, 0:D]).then_inc(dve_emptied, 1)
                    return
                last = w - 1
                rows = outs[:, last, :] if isinstance(last, int) else outs[:, bass.ds(last, 1), :].rearrange("p o d -> p (o d)")
                nc.vector.tensor_copy(rows, bd[1][:, 0:D]).then_inc(dve_emptied, 1)

            nc.vector.memset(csum[:], 0.0).then_inc(csum_ready, 1)
            window(0, False)
            window(1, True)
            with dve.Fori(2, WINDOWS - 1) as w:
                window(w, True)
            window(WINDOWS - 1, True, final=True)
            add_up_behind(WINDOWS, 0)
            add_up(WINDOWS - 1, STEPS - 1)
            dve.wait_ge(ctx_done, WINDOWS)
            pick_part(0)
            dve.wait_ge(ctx_read, WINDOWS * 3)
            nc.vector.tensor_reduce(csum[:, 0:D], picked[:].rearrange("p k d -> p d k"), AX_X, ALU.add).then_inc(csum_ready, 1)
            n = WINDOWS * DVE_N
            dve.wait_ge(dve_filled, n + 1)
            nc.vector.tensor_copy(csum_t[0:D, :], ba[0][0:D, 0:P]).then_inc(dve_emptied, 1)
            dve.wait_ge(dve_filled, n + 2)
            nc.vector.tensor_copy(outs[:, WINDOWS - 1, :], ba[1][:, 0:D]).then_inc(window_done, 1)

        @block.tensor
        def _(pe):
            pe.wait_ge(weights_loaded, 16)
            nc.tensor.matmul(ba[1][0:D, 0:D], w_s[:, 0, :], w_s[:, 1, :], start=True, stop=True)
            nc.tensor.matmul(ba[1][0:D, D:2 * D], w_s[:, 2, :], w_s[:, 3, :], start=True, stop=True).then_inc(prep_pe, 1)
            pe.wait_ge(prep_done, 1)
            pe.wait_ge(tgt_t_loaded, 16)
            for q, b in enumerate((ba[0], bd[0], bd[1])):
                nc.tensor.matmul(b[:], m_score[:].rearrange("p o d -> p (o d)"),
                                 tgt_t[:, q * 512:(q + 1) * 512], start=True, stop=True).then_inc(prep_pe, 1)
                if q == 0:
                    for k in range(DIRECT):
                        rows = (WINDOWS + k) * P
                        op = nc.tensor.matmul(ba[1][:, P + k * D:P + (k + 1) * D], tgt_t[:, rows:rows + P], m_score[:, 0, :],
                                              start=True, stop=True)
                    op.then_inc(prep_pe, 1)

            def score(w, s, q):
                if q == 0:
                    for half in range(2):
                        pe.wait_ge(loaded[s][half], (w + 1) * 16)
                if s == 0 and q == 0:
                    pe.wait_ge(g_placed, 2 * w + 1)
                    ge(pe, masked_done, w)
                if s == 2 and q == 0:
                    pe.wait_ge(g_placed, 2 * w + 2)
                for t in range(TILES):
                    r = nc.tensor.matmul(ps_score[t * COLS:(t + 1) * COLS, 0:2 * L], g_cols[:, t, s, q, :],
                                         hist[:, s, t, q, :],
                                         start=(s == 0 and q == 0), stop=(s == STEPS - 1 and q == 1),
                                         tile_position=(0, t * COLS))
                if s == STEPS - 1 and q == 1:
                    r.then_inc(scored, 1)

            def sum0(w, s):
                pe.wait_ge(act_emptied, (w - 1) * ACT_N + index(ACT_FILLS, "F3", s) + 1)
                for t in range(TILES):
                    r = nc.tensor.matmul(ps_c0[t * COLS:(t + 1) * COLS, :], w0[:, t, s, :], h0[:, s, t, :],
                                     start=(s == 0), stop=(s == STEPS - 1), tile_position=(0, t * COLS))
                return r

            def sum1(w, j):
                pe.wait_ge(act_emptied, (w - 1) * ACT_N + index(ACT_FILLS, "F4", 2 * j + 1) + 1)
                pe.wait_ge(dve_emptied, (w - 1) * DVE_N + index(DVE_FILLS, "F5", 2 * j + 1) + 1)
                for t in range(TILES):
                    r = nc.tensor.matmul(ps_c1[t * COLS:(t + 1) * COLS, :], w1[:, j, t, :],
                                     h1[:, t, 2 * j:2 * j + 2, :].rearrange("p s n -> p (s n)"),
                                     start=(j == 0), stop=(j == 1), tile_position=(0, t * COLS))
                return r

            def sum_rest(w):
                pe.wait_ge(act_emptied, w * ACT_N)
                for t in range(TILES):
                    r = nc.tensor.matmul(ps_cr[t * COLS:(t + 1) * COLS, :], wr[:, t, :], hr[:, t, :],
                                         start=True, stop=True, tile_position=(0, t * COLS))
                return r

            def before_sums(w):
                pe.wait_ge(weights_placed, w)

            def free(w, fills, n, emptied, banks, name, s):
                i = index(fills, name, s)
                b = fills[i][2]
                last = max(k for k in range(-n, i) if fills[k % n][2] == b)
                ge(pe, emptied, w * n + last + 1)
                return banks[b]

            def act_bank(w, name, s):
                return free(w, ACT_FILLS, ACT_N, act_emptied, ba, name, s)

            def dve_bank(w, name, s):
                return free(w, DVE_FILLS, DVE_N, dve_emptied, bd, name, s)

            def turn0(w, s, t):
                ps = act_bank(w, f"F{t}", s)
                for r in range(PAIRS):
                    op = nc.tensor.transpose(ps[:, r * P:(r + 1) * P], hist[:, s, t, r // 2, r % 2 * L0:(r % 2 + 1) * L0], ident)
                op.then_inc(act_filled, 1)

            def turn1(w, s, half):
                if not half:
                    pe.wait_ge(rest_copied, w * STEPS + s + 1)
                ps = dve_bank(w, "F5", s) if half else act_bank(w, "F4", s)
                for k in range(4):
                    t, c = 2 * half + k // 2, k % 2
                    op = nc.tensor.transpose(ps[:, k * P:(k + 1) * P], hist[:, s, t, c, 2 * L0:2 * (L0 + L1)], ident)
                op.then_inc(dve_filled if half else act_filled, 1)

            def turn_rest(w):
                pe.wait_ge(rest_copied, (w + 1) * STEPS)
                ps = act_bank(w, "FR", STEPS - 1)
                for t in range(TILES):
                    op = nc.tensor.transpose(ps[:, t * P:(t + 1) * P], rest[:, t, :, :].rearrange("p r l -> p (r l)"), ident)
                op.then_inc(act_filled, 1)

            def turn_weights(w):
                pe.wait_ge(att_ready, w + 1)
                ge(pe, ctx_read, w * 3)
                for k in range(len(CUTS)):
                    op = nc.tensor.transpose(ps_at[:, k * P:(k + 1) * P], att[:, k * P:(k + 1) * P], ident)
                op.then_inc(at_done, 1)

            def csum_turn(w, b):
                pe.wait_ge(csum_ready, w + 1)
                nc.tensor.transpose(b[:, 0:P], csum[:], ident).then_inc(dve_filled, 1)

            def out_product(w, b, emptied):
                pe.wait_ge(tgt_placed, w + 1)
                pe.wait_ge(dve_emptied, emptied)
                nc.tensor.matmul(b[:, 0:D], csum_t[:], m_out[:], start=True, stop=True).then_inc(dve_filled, 1)

            def window(w, sums, more):
                for s in range(STEPS):
                    last = s == STEPS - 1
                    ahead = (lambda q: score(w, s + 1, q)) if not last else (lambda q: score(w + 1, 0, q))
                    if sums:
                        if s == 0:
                            before_sums(w)
                            sum0(w, 0)
                        elif s == 1:
                            sum0(w, 1)
                            sum0(w, 2)
                        elif s == 2:
                            sum1(w, 1)
                            sum_rest(w).then_inc(ctx_done, 1)
                    turn0(w, s, 0)
                    turn0(w, s, 1)
                    if sums:
                        if s == 0:
                            sum1(w, 0)
                        elif s == 1:
                            sum0(w, 3)
                    if s >= EARLY_F5:
                        turn1(w, s, 1)
                    if last:
                        csum_turn(w, dve_bank(w, "CT", s))
                    turn1(w, s, 0)
                    turn0(w, s, 2)
                    if last:
                        turn_weights(w)
                    if more or not last:
                        ahead(0)
                    turn0(w, s, 3)
                    if s < EARLY_F5:
                        turn1(w, s, 1)
                    if last:
                        out_product(w, dve_bank(w, "OUT", s), w * DVE_N + index(DVE_FILLS, "CT", s) + 1)
                        turn_rest(w)
                    if more or not last:
                        ahead(1)

            score(0, 0, 0)
            score(0, 0, 1)
            pe.wait_ge(prep_done, 5)
            pe.wait_ge(const_loaded, 16)
            window(0, False, True)
            with pe.Fori(1, WINDOWS - 1) as w:
                window(w, True, True)
            window(WINDOWS - 1, True, False)
            w = WINDOWS
            before_sums(w)
            sum1(w, 0)
            sum1(w, 1).then_inc(ctx_late_done, 1)
            sum_rest(w).then_inc(ctx_late_done, 1)
            for s in range(STEPS):
                op = sum0(w, s)
            op.then_inc(ctx_done, 1)
            pe.wait_ge(dsum_done, DIRECT)
            pe.wait_ge(dve_emptied, w * DVE_N)
            for k in range(DIRECT - 1):
                nc.tensor.transpose(bd[0][0:D, k * P:(k + 1) * P], dsum[:, k, :], ident)
            last_block = bd[0][0:D, (DIRECT - 1) * P:DIRECT * P]
            nc.tensor.matmul(last_block, dsum[:, DIRECT - 1, :], ident, start=True, stop=False)
            for s in range(STEPS):
                pe.wait_ge(part_done, CHUNKS - STEPS + s + 1)
                op = nc.tensor.matmul(last_block, parts[:, WINDOWS - 1, s, :], ident, start=False, stop=(s == STEPS - 1))
            op.then_inc(dsum_turned, 1)
            pe.wait_ge(dsum_copied, 1)
            for k in range(DIRECT):
                op = nc.tensor.matmul(bd[1][:, k * D:(k + 1) * D], dsum_t[:, k, :], m_out[:], start=True, stop=True)
            op.then_inc(dproduct_done, 1)
            csum_turn(w, ba[0])
            out_product(w, ba[1], w * DVE_N + 1)


def constants():
    import numpy as np
    c = np.zeros((P, C_END), np.float32)
    p = np.arange(P)
    c[:, C_ID:C_ID + P] = np.eye(P)
    b = p % COLS
    s, pr, par = b // 8, b // 2 % PAIRS, b % 2
    c[p, C_SELS + pr % 2] = 1
    c[p, C_SELC + pr * 2 + par] = 1
    c[p, C_SELD + (s % 2) * 4 + (pr // 2) * 2 + par] = 1
    c[p, C_SELE + par] = 1
    col = np.arange(COLS)
    for j in range(2):
        c[:, C_SEL1 + j * COLS:C_SEL1 + (j + 1) * COLS] = (col // 16 == j) & (col // 2 % 2 == (p // L1)[:, None])
    c[:, C_SELR:C_SELR + COLS] = col // 2 == (p // LR)[:, None]
    return c


def kernel(**inputs):
    import numpy as np
    import concourse.bacc as bacc
    from concourse.bass_utils import run_bass_kernel_spmd

    nc = bacc.Bacc("TRN2", target_bir_lowering=False, num_devices=1)
    history = np.asarray(inputs["r_history_sequence"])
    hist = history[:WINDOWS * P].reshape(WINDOWS, TILES, STEPS, 2, 2, PAR, L, D)
    hist = hist.transpose(0, 2, 5, 7, 1, 3, 4, 6)
    laid, at = [], 0
    for _, n in CUTS:
        laid.append(hist[..., at:at + n].reshape(WINDOWS * STEPS, P, TILES, 2, 2 * n))
        at += n
    hist = np.concatenate(laid, axis=-1).reshape(WINDOWS * STEPS, P, 2, TILES * 2 * L)
    hist = np.ascontiguousarray(hist.transpose(0, 2, 1, 3))
    direct = np.zeros((DIRECT, P, BLOCK_WINDOWS * BESIDE, D), history.dtype)
    direct[:, :, :L] = history[WINDOWS * P:].reshape(DIRECT, P, L, D)
    direct = direct.reshape(DIRECT, P, BLOCK_WINDOWS, BESIDE * D).transpose(0, 2, 1, 3)
    mask = np.asarray(inputs["r_mask"]).reshape(B, L)
    direct_mask = np.zeros((DIRECT, P, BLOCK_WINDOWS * BESIDE), mask.dtype)
    direct_mask[:, :, :L] = mask[WINDOWS * P:].reshape(DIRECT, P, L)
    direct_mask = direct_mask.transpose(1, 0, 2)
    target = np.asarray(inputs["r_target_item"]).reshape(B, D)
    wq, wk, wv, wo = (np.asarray(inputs[f"L0_rec_W_{x}"]) for x in "qkvo")
    weights = np.stack([wq.T, wk.T, wv.T, wo], axis=1)
    arrays = {
        "target_t": np.ascontiguousarray(target.T),
        "history": hist,
        "direct": np.ascontiguousarray(direct).reshape(WINDOWS, P, BESIDE * D),
        "mask": np.ascontiguousarray(mask),
        "direct_mask": np.ascontiguousarray(direct_mask).reshape(P, WINDOWS * BESIDE),
        "weights": np.ascontiguousarray(weights).reshape(A, 4 * D),
        "consts": constants(),
    }
    args = [nc.dram_tensor(n, a.shape, mybir.dt.from_np(a.dtype), kind="ExternalInput").ap() for n, a in arrays.items()]
    out = nc.dram_tensor("out", (P, BLOCKS * D), F32, kind="ExternalOutput").ap()
    attention_kernel(nc, *args, out)
    r = run_bass_kernel_spmd(nc, [arrays], core_ids=[0])
    return np.ascontiguousarray(r.results[0]["out"].reshape(P, BLOCKS, D).transpose(1, 0, 2)).reshape(B, D)
```
